# Optimizing a Trainium2 kernel written in Bass

```python
import numpy as np
import jax
import jax.numpy as jnp

def _softmax(x, axis=-1):
    return jax.nn.softmax(x, axis=axis)

def _gelu(x):
    return jax.nn.gelu(x, approximate=True)

def _silu(x):
    return jax.nn.silu(x)

def _sigmoid(x):
    return jax.nn.sigmoid(x)

def _layernorm(x, axis=-1, eps=1e-05):
    m = jnp.mean(x, axis=axis, keepdims=True)
    v = jnp.var(x, axis=axis, keepdims=True)
    return (x - m) / jnp.sqrt(v + eps)

def _scatter_add(tgt, idx, src, axis=0):
    return tgt.at[idx].add(src)

def _segment_sum(src, seg, n):
    return jax.ops.segment_sum(src, seg, n)
kernel_name = 'mk_decoder_preln_d2_seqx_r8_a7032a'

def setup_inputs(seed: int=0):
    np.random.seed(seed)
    _w = jnp.asarray

    def _rec_inputs():
        import jax
        import jax.numpy as jnp
        _rk = jax.random.key(seed)
        x = 7.22e-05 + 1 * jax.random.normal(jax.random.fold_in(_rk, 1), (64, 64, 128), jnp.float32)
        _lenS = 64 - jax.random.randint(jax.random.fold_in(_rk, 7), (64,), 0, max(1, 64 // 4) + 1, jnp.int32)
        _lenS2 = 64 - jax.random.randint(jax.random.fold_in(_rk, 8), (64,), 0, max(1, 64 // 4) + 1, jnp.int32)
        _ctx_1024P = jax.random.normal(jax.random.fold_in(_rk, 11), (64, 16, 128), jnp.float32)
        _ctx_1024c = jax.random.dirichlet(jax.random.fold_in(_rk, 511), 0.3 * jnp.ones((16,), jnp.float32), (64, 64))
        _ctx_1024t = jnp.einsum('bsk,bkd->bsd', _ctx_1024c, _ctx_1024P)
        _ctx_1024t = _ctx_1024t * jax.lax.rsqrt(jnp.mean(jnp.square(_ctx_1024t)) + 1e-12) * 0.953939
        ctx_1024 = 4.13588e-05 + 0.999923 * (_ctx_1024t + 0.3 * jax.random.normal(jax.random.fold_in(_rk, 611), (64, 64, 128), jnp.float32))
        return (x, ctx_1024)
    x, ctx_1024 = _rec_inputs()

    def _L0_attn_setup():
        import jax, jax.numpy as jnp
        import numpy as np
        B, S, D = (4, 256, 128)
        H, DH = (16, 64)
        key = jax.random.key(seed)
        kx, kq, kk, kv, ko = jax.random.split(key, 5)
        scale = 1.0 / np.sqrt(D)
        return {'x': jax.random.normal(kx, (B, S, D), dtype=jnp.float32), 'Wq': jax.random.normal(kq, (D, H * DH), dtype=jnp.float32) * scale, 'Wk': jax.random.normal(kk, (D, H * DH), dtype=jnp.float32) * scale, 'Wv': jax.random.normal(kv, (D, H * DH), dtype=jnp.float32) * scale, 'Wo': jax.random.normal(ko, (H * DH, D), dtype=jnp.float32) * scale}
    _L0_attn_all = _L0_attn_setup()
    _L0_attn_in = {k: v for k, v in _L0_attn_all.items() if k in ('Wq', 'Wk', 'Wv', 'Wo')}
    del _L0_attn_all

    def _L0_xattn_setup():
        import jax, jax.numpy as jnp
        import numpy as np
        D_MODEL = 128
        NUM_HEADS = 16
        DEPTH = D_MODEL // NUM_HEADS

        def _split_heads(x, B, S):
            return x.reshape(B, S, NUM_HEADS, DEPTH).transpose(0, 2, 1, 3)
        key = jax.random.key(seed)
        ks = jax.random.split(key, 11)
        B, S = (4, 256)
        scale = 1.0 / np.sqrt(D_MODEL)
        inp = {'q': jax.random.normal(ks[0], (B, S, D_MODEL), jnp.float32), 'k': jax.random.normal(ks[1], (B, S, D_MODEL), jnp.float32), 'v': jax.random.normal(ks[2], (B, S, D_MODEL), jnp.float32), 'wq_w': jax.random.normal(ks[3], (D_MODEL, D_MODEL), jnp.float32) * scale, 'wq_b': jnp.zeros((D_MODEL,), jnp.float32), 'wk_w': jax.random.normal(ks[4], (D_MODEL, D_MODEL), jnp.float32) * scale, 'wk_b': jnp.zeros((D_MODEL,), jnp.float32), 'wv_w': jax.random.normal(ks[5], (D_MODEL, D_MODEL), jnp.float32) * scale, 'wv_b': jnp.zeros((D_MODEL,), jnp.float32), 'wo_w': jax.random.normal(ks[6], (D_MODEL, D_MODEL), jnp.float32) * scale, 'wo_b': jnp.zeros((D_MODEL,), jnp.float32)}
        return inp
    _L0_xattn_all = _L0_xattn_setup()
    _L0_xattn_in = {k: v for k, v in _L0_xattn_all.items() if k in ('wq_w', 'wq_b', 'wk_w', 'wk_b', 'wv_w', 'wv_b', 'wo_w', 'wo_b')}
    del _L0_xattn_all

    def _L0_ffn_setup():
        import jax, jax.numpy as jnp
        import numpy as np
        S, B, H, I, E = (64, 2, 128, 352, 8)
        key = jax.random.key(seed)
        ks = jax.random.split(key, 5)
        return {'hidden_states': jax.random.normal(ks[0], (S, B, H), dtype=jnp.float32), 'router_w': jax.random.normal(ks[1], (E, H), dtype=jnp.float32) * 0.02, 'gate_w': jax.random.normal(ks[2], (E, I, H), dtype=jnp.float32) * 0.02, 'up_w': jax.random.normal(ks[3], (E, I, H), dtype=jnp.float32) * 0.02, 'down_w': jax.random.normal(ks[4], (E, H, I), dtype=jnp.float32) * 0.02}
    _L0_ffn_all = _L0_ffn_setup()
    _L0_ffn_in = {k: v for k, v in _L0_ffn_all.items() if k in ('router_w', 'gate_w', 'up_w', 'down_w')}
    del _L0_ffn_all

    def _L1_attn_setup():
        import jax, jax.numpy as jnp
        import numpy as np
        EPS = 1e-06
        DECAY = 0.9
        THR = 0.5
        SBETA = 10.0
        KW = 4

        def _rms(x, w):
            return x * jax.lax.rsqrt(jnp.mean(x * x, axis=-1, keepdims=True) + EPS) * w
        B, T, D, H, dk, dv, r, dff = (2, 256, 128, 8, 64, 64, 64, 512)
        keys = iter(jax.random.split(jax.random.key(seed), 24))

        def g(shape, s=0.02):
            return jax.random.normal(next(keys), shape, jnp.float32) * s
        return {'x': jax.random.normal(next(keys), (B, T, D), jnp.float32), 'norm_in_w': jnp.ones((D,), jnp.float32), 'conv_w': g((D, 1, KW), 0.3), 'conv_b': jnp.zeros((D,), jnp.float32), 'Wq': g((D, H * dk)), 'Wk': g((D, H * dk)), 'Wv': g((D, H * dv)), 'Wo': g((H * dv, D)), 'Wspike': g((D, H * dk), 0.1), 'Wau': g((D, r)), 'bau': jnp.zeros((r,), jnp.float32), 'Wad': g((r, H * dk)), 'bad': jnp.zeros((H * dk,), jnp.float32), 'alpha_spike': jnp.zeros((1, H, dk), jnp.float32), 'Wbeta': g((D, H)), 'bbeta': jnp.zeros((H,), jnp.float32), 'beta_spike': jnp.zeros((1, H, dk), jnp.float32), 'head_norm_w': jnp.ones((H, dv), jnp.float32), 'Wu1': g((D, r)), 'bu1': jnp.zeros((r,), jnp.float32), 'Wu2': g((r, D)), 'bu2': jnp.zeros((D,), jnp.float32), 'ff_norm_w': jnp.ones((D,), jnp.float32), 'Wff1': g((D, dff)), 'Wff3': g((D, dff)), 'Wff2': g((dff, D))}
    _L1_attn_all = _L1_attn_setup()
    _L1_attn_in = {k: v for k, v in _L1_attn_all.items() if k in ('norm_in_w', 'conv_w', 'conv_b', 'Wq', 'Wk', 'Wv', 'Wo', 'Wspike', 'Wau', 'bau', 'Wad', 'bad', 'alpha_spike', 'Wbeta', 'bbeta', 'beta_spike', 'head_norm_w', 'Wu1', 'bu1', 'Wu2', 'bu2', 'ff_norm_w', 'Wff1', 'Wff3', 'Wff2')}
    del _L1_attn_all

    def _L1_xattn_setup():
        import jax, jax.numpy as jnp
        import numpy as np
        B, S, H, NH = (2, 256, 128, 4)
        DH = H // NH
        EPS = 1e-06

        def _parallel_stabilized(qh, kh, vh, ig, fg):
            log_fg = jax.nn.log_sigmoid(fg)
            cs = jnp.cumsum(log_fg, axis=2)
            ltr = jnp.tril(jnp.ones((qh.shape[2], qh.shape[2]), dtype=bool))
            log_fg_mat = jnp.where(ltr, cs - jnp.swapaxes(cs, 2, 3), -jnp.inf)
            log_D = log_fg_mat + jnp.swapaxes(ig, 2, 3)
            max_log_D = jnp.max(log_D, axis=-1, keepdims=True)
            D = jnp.exp(log_D - max_log_D)
            qk = jnp.einsum('bhsd,bhtd->bhst', qh, kh) / jnp.sqrt(jnp.float32(DH))
            C = qk * D
            normalizer = jnp.maximum(jnp.abs(jnp.sum(C, axis=-1, keepdims=True)), jnp.exp(-max_log_D))
            return jnp.einsum('bhst,bhtd->bhsd', C / (normalizer + EPS), vh)
        key = jax.random.key(seed)
        ks = jax.random.split(key, 6)
        q = jax.random.normal(ks[0], (B, S, H), dtype=jnp.float32)
        k = jax.random.normal(ks[1], (B, S, H), dtype=jnp.float32)
        v = jax.random.normal(ks[2], (B, S, H), dtype=jnp.float32)
        igate_kernel = jax.random.normal(ks[3], (3 * H, NH), dtype=jnp.float32) * 0.02
        fgate_kernel = jax.random.normal(ks[4], (3 * H, NH), dtype=jnp.float32) * 0.02
        igate_bias = jax.random.normal(ks[5], (NH,), dtype=jnp.float32) * 0.1
        fgate_bias = jnp.linspace(3.0, 6.0, NH, dtype=jnp.float32)
        outnorm_scale = jnp.ones((H,), dtype=jnp.float32)
        return {'q': q, 'k': k, 'v': v, 'igate_kernel': igate_kernel, 'igate_bias': igate_bias, 'fgate_kernel': fgate_kernel, 'fgate_bias': fgate_bias, 'outnorm_scale': outnorm_scale}
    _L1_xattn_all = _L1_xattn_setup()
    _L1_xattn_in = {k: v for k, v in _L1_xattn_all.items() if k in ('igate_kernel', 'igate_bias', 'fgate_kernel', 'fgate_bias', 'outnorm_scale')}
    del _L1_xattn_all

    def _L1_ffn_setup():
        import jax, jax.numpy as jnp
        import numpy as np
        E = 8
        TOP_K = 2
        LN_EPS = 1e-05

        def _layernorm(x, g, b):
            mu = jnp.mean(x, axis=-1, keepdims=True)
            var = jnp.var(x, axis=-1, keepdims=True)
            return (x - mu) * jax.lax.rsqrt(var + LN_EPS) * g + b
        key = jax.random.key(seed)
        ks = jax.random.split(key, 4)
        B, T, H, HF = (4, 256, 128, 256)
        s_in = 1.0 / np.sqrt(H)
        s_hid = 1.0 / np.sqrt(HF)
        return {'x': jax.random.normal(ks[0], (B, T, H), dtype=jnp.float32), 'ln_g': jnp.ones((H,), dtype=jnp.float32), 'ln_b': jnp.zeros((H,), dtype=jnp.float32), 'rW': jax.random.normal(ks[1], (H, E), dtype=jnp.float32) * s_in, 'rb': jnp.zeros((E,), dtype=jnp.float32), 'W1': jax.random.normal(ks[2], (E, H, HF), dtype=jnp.float32) * s_in, 'b1': jnp.zeros((E, HF), dtype=jnp.float32), 'W2': jax.random.normal(ks[3], (E, HF, H), dtype=jnp.float32) * s_hid, 'b2': jnp.zeros((E, H), dtype=jnp.float32)}
    _L1_ffn_all = _L1_ffn_setup()
    _L1_ffn_in = {k: v for k, v in _L1_ffn_all.items() if k in ('ln_g', 'ln_b', 'rW', 'rb', 'W1', 'b1', 'W2', 'b2')}
    del _L1_ffn_all
    return {'x': x, 'ctx_1024': ctx_1024, 'L0_attn_Wq': _L0_attn_in['Wq'], 'L0_attn_Wk': _L0_attn_in['Wk'], 'L0_attn_Wv': _L0_attn_in['Wv'], 'L0_attn_Wo': _L0_attn_in['Wo'], 'L0_xattn_wq_w': _L0_xattn_in['wq_w'], 'L0_xattn_wq_b': _L0_xattn_in['wq_b'], 'L0_xattn_wk_w': _L0_xattn_in['wk_w'], 'L0_xattn_wk_b': _L0_xattn_in['wk_b'], 'L0_xattn_wv_w': _L0_xattn_in['wv_w'], 'L0_xattn_wv_b': _L0_xattn_in['wv_b'], 'L0_xattn_wo_w': _L0_xattn_in['wo_w'], 'L0_xattn_wo_b': _L0_xattn_in['wo_b'], 'L0_ffn_router_w': _L0_ffn_in['router_w'], 'L0_ffn_gate_w': _L0_ffn_in['gate_w'], 'L0_ffn_up_w': _L0_ffn_in['up_w'], 'L0_ffn_down_w': _L0_ffn_in['down_w'], 'L1_attn_norm_in_w': _L1_attn_in['norm_in_w'], 'L1_attn_conv_w': _L1_attn_in['conv_w'], 'L1_attn_conv_b': _L1_attn_in['conv_b'], 'L1_attn_Wq': _L1_attn_in['Wq'], 'L1_attn_Wk': _L1_attn_in['Wk'], 'L1_attn_Wv': _L1_attn_in['Wv'], 'L1_attn_Wo': _L1_attn_in['Wo'], 'L1_attn_Wspike': _L1_attn_in['Wspike'], 'L1_attn_Wau': _L1_attn_in['Wau'], 'L1_attn_bau': _L1_attn_in['bau'], 'L1_attn_Wad': _L1_attn_in['Wad'], 'L1_attn_bad': _L1_attn_in['bad'], 'L1_attn_alpha_spike': _L1_attn_in['alpha_spike'], 'L1_attn_Wbeta': _L1_attn_in['Wbeta'], 'L1_attn_bbeta': _L1_attn_in['bbeta'], 'L1_attn_beta_spike': _L1_attn_in['beta_spike'], 'L1_attn_head_norm_w': _L1_attn_in['head_norm_w'], 'L1_attn_Wu1': _L1_attn_in['Wu1'], 'L1_attn_bu1': _L1_attn_in['bu1'], 'L1_attn_Wu2': _L1_attn_in['Wu2'], 'L1_attn_bu2': _L1_attn_in['bu2'], 'L1_attn_ff_norm_w': _L1_attn_in['ff_norm_w'], 'L1_attn_Wff1': _L1_attn_in['Wff1'], 'L1_attn_Wff3': _L1_attn_in['Wff3'], 'L1_attn_Wff2': _L1_attn_in['Wff2'], 'L1_xattn_igate_kernel': _L1_xattn_in['igate_kernel'], 'L1_xattn_igate_bias': _L1_xattn_in['igate_bias'], 'L1_xattn_fgate_kernel': _L1_xattn_in['fgate_kernel'], 'L1_xattn_fgate_bias': _L1_xattn_in['fgate_bias'], 'L1_xattn_outnorm_scale': _L1_xattn_in['outnorm_scale'], 'L1_ffn_ln_g': _L1_ffn_in['ln_g'], 'L1_ffn_ln_b': _L1_ffn_in['ln_b'], 'L1_ffn_rW': _L1_ffn_in['rW'], 'L1_ffn_rb': _L1_ffn_in['rb'], 'L1_ffn_W1': _L1_ffn_in['W1'], 'L1_ffn_b1': _L1_ffn_in['b1'], 'L1_ffn_W2': _L1_ffn_in['W2'], 'L1_ffn_b2': _L1_ffn_in['b2']}

def reference(x, ctx_1024, L0_attn_Wq, L0_attn_Wk, L0_attn_Wv, L0_attn_Wo, L0_xattn_wq_w, L0_xattn_wq_b, L0_xattn_wk_w, L0_xattn_wk_b, L0_xattn_wv_w, L0_xattn_wv_b, L0_xattn_wo_w, L0_xattn_wo_b, L0_ffn_router_w, L0_ffn_gate_w, L0_ffn_up_w, L0_ffn_down_w, L1_attn_norm_in_w, L1_attn_conv_w, L1_attn_conv_b, L1_attn_Wq, L1_attn_Wk, L1_attn_Wv, L1_attn_Wo, L1_attn_Wspike, L1_attn_Wau, L1_attn_bau, L1_attn_Wad, L1_attn_bad, L1_attn_alpha_spike, L1_attn_Wbeta, L1_attn_bbeta, L1_attn_beta_spike, L1_attn_head_norm_w, L1_attn_Wu1, L1_attn_bu1, L1_attn_Wu2, L1_attn_bu2, L1_attn_ff_norm_w, L1_attn_Wff1, L1_attn_Wff3, L1_attn_Wff2, L1_xattn_igate_kernel, L1_xattn_igate_bias, L1_xattn_fgate_kernel, L1_xattn_fgate_bias, L1_xattn_outnorm_scale, L1_ffn_ln_g, L1_ffn_ln_b, L1_ffn_rW, L1_ffn_rb, L1_ffn_W1, L1_ffn_b1, L1_ffn_W2, L1_ffn_b2):
    import jax
    import jax.numpy as jnp

    def _L0_attn_ref(x, Wq, Wk, Wv, Wo):
        import jax, jax.numpy as jnp
        import numpy as np
        B, S, D = (4, 256, 128)
        H, DH = (16, 64)
        b, s, _ = x.shape
        q = (x @ Wq).reshape(b, s, H, DH).transpose(0, 2, 1, 3)
        k = (x @ Wk).reshape(b, s, H, DH).transpose(0, 2, 1, 3)
        v = (x @ Wv).reshape(b, s, H, DH).transpose(0, 2, 1, 3)
        logits = jnp.einsum('bhqd,bhkd->bhqk', q, k) / jnp.sqrt(jnp.float32(DH))
        mask = jnp.triu(jnp.ones((s, s), dtype=bool), k=1)
        logits = jnp.where(mask, -jnp.inf, logits)
        probs = jax.nn.softmax(logits, axis=-1)
        attn = jnp.einsum('bhqk,bhkd->bhqd', probs, v)
        attn = attn.transpose(0, 2, 1, 3).reshape(b, s, H * DH)
        return attn @ Wo

    def _L0_xattn_ref(q, k, v, wq_w, wq_b, wk_w, wk_b, wv_w, wv_b, wo_w, wo_b):
        import jax, jax.numpy as jnp
        import numpy as np
        D_MODEL = 128
        NUM_HEADS = 16
        DEPTH = D_MODEL // NUM_HEADS

        def _split_heads(x, B, S):
            return x.reshape(B, S, NUM_HEADS, DEPTH).transpose(0, 2, 1, 3)
        B, S, _ = q.shape
        qh = _split_heads(q @ wq_w.T + wq_b, B, S)
        kh = _split_heads(k @ wk_w.T + wk_b, B, S)
        vh = _split_heads(v @ wv_w.T + wv_b, B, S)
        scores = jnp.einsum('bhqd,bhkd->bhqk', qh, kh) / jnp.sqrt(jnp.asarray(DEPTH, qh.dtype))
        attn = jax.nn.softmax(scores, axis=-1)
        ctx = jnp.einsum('bhqk,bhkd->bhqd', attn, vh)
        ctx = ctx.transpose(0, 2, 1, 3).reshape(B, S, D_MODEL)
        return ctx @ wo_w.T + wo_b

    def _L0_ffn_ref(hidden_states, router_w, gate_w, up_w, down_w):
        import jax, jax.numpy as jnp
        import numpy as np
        S, B, H, I, E = (64, 2, 128, 352, 8)
        router_logits = jnp.einsum('sbh,eh->sbe', hidden_states, router_w)
        routing_indices = jnp.argmax(router_logits, axis=-1)
        out = jnp.zeros_like(hidden_states)
        for e in range(E):
            mask = (routing_indices == e)[..., None]
            xe = jnp.where(mask, hidden_states, 0.0)
            g = jnp.einsum('sbh,ih->sbi', xe, gate_w[e])
            u = jnp.einsum('sbh,ih->sbi', xe, up_w[e])
            ye = jnp.einsum('sbi,hi->sbh', jax.nn.silu(g) * u, down_w[e])
            out = out + jnp.where(mask, ye, 0.0)
        return out

    def _L1_attn_ref(x, norm_in_w, conv_w, conv_b, Wq, Wk, Wv, Wo, Wspike, Wau, bau, Wad, bad, alpha_spike, Wbeta, bbeta, beta_spike, head_norm_w, Wu1, bu1, Wu2, bu2, ff_norm_w, Wff1, Wff3, Wff2):
        import jax, jax.numpy as jnp
        import numpy as np
        EPS = 1e-06
        DECAY = 0.9
        THR = 0.5
        SBETA = 10.0
        KW = 4

        def _rms(x, w):
            return x * jax.lax.rsqrt(jnp.mean(x * x, axis=-1, keepdims=True) + EPS) * w
        B, T, D = x.shape
        H, dk = (alpha_spike.shape[1], alpha_spike.shape[2])
        dv = head_norm_w.shape[1]
        h = _rms(x, norm_in_w)
        hc = jnp.transpose(h, (0, 2, 1))
        conv = jax.lax.conv_general_dilated(hc, conv_w, window_strides=(1,), padding=[(KW - 1, 0)], dimension_numbers=('NCH', 'OIH', 'NCH'), feature_group_count=D)
        conv = conv + conv_b[None, :, None]
        h = jax.nn.silu(jnp.transpose(conv, (0, 2, 1)))

        def heads(z, d):
            return z.reshape(B, T, H, d)
        q = heads(h @ Wq, dk)
        k = heads(h @ Wk, dk)
        v = heads(h @ Wv, dv)
        q = q / (jnp.linalg.norm(q, axis=-1, keepdims=True) + 1e-06)
        k = k / (jnp.linalg.norm(k, axis=-1, keepdims=True) + 1e-06)
        drive = heads(h @ Wspike, dk)
        alpha_base = heads(jax.nn.silu(h @ Wau + bau) @ Wad + bad, dk)
        beta_base = h @ Wbeta + bbeta
        asp = alpha_spike[0]
        bsp = beta_spike[0]

        def step(carry, ins):
            s, mem = carry
            qt, kt, vt, dt, at, bt = ins
            mem = DECAY * mem + dt
            sg = jax.nn.sigmoid(SBETA * (mem - THR))
            hard = (mem > THR).astype(mem.dtype)
            spike = sg + jax.lax.stop_gradient(hard - sg)
            mem = mem - spike * THR
            alpha = jax.nn.sigmoid(at + asp * spike)
            beta = jax.nn.sigmoid(bt[..., None] + jnp.sum(spike * bsp, -1, keepdims=True))
            active = (jnp.sum(jnp.abs(spike), -1, keepdims=True) > 0).astype(qt.dtype)
            alpha = jnp.where(active > 0, alpha, jnp.ones_like(alpha))
            beta = beta * active
            s = s * alpha[..., None]
            pred = jnp.einsum('bhk,bhkv->bhv', kt, s)
            s = s + (beta * kt)[..., None] * (vt - pred)[:, :, None, :]
            out = jnp.einsum('bhk,bhkv->bhv', qt, s)
            return ((s, mem), out)
        s0 = jnp.zeros((B, H, dk, dv), x.dtype)
        m0 = jnp.zeros((B, H, dk), x.dtype)
        xs = (jnp.moveaxis(q, 1, 0), jnp.moveaxis(k, 1, 0), jnp.moveaxis(v, 1, 0), jnp.moveaxis(drive, 1, 0), jnp.moveaxis(alpha_base, 1, 0), jnp.moveaxis(beta_base, 1, 0))
        _, y = jax.lax.scan(step, (s0, m0), xs)
        y = jnp.moveaxis(y, 0, 1)
        y = y * jax.lax.rsqrt(jnp.mean(y * y, axis=-1, keepdims=True) + EPS) * head_norm_w
        y = y.reshape(B, T, H * dv)
        gate = jax.nn.sigmoid(jax.nn.silu(x @ Wu1 + bu1) @ Wu2 + bu2)
        y = x + y @ Wo * gate
        z = _rms(y, ff_norm_w)
        y = y + jax.nn.silu(z @ Wff1) * (z @ Wff3) @ Wff2
        return y

    def _L1_xattn_ref(q, k, v, igate_kernel, igate_bias, fgate_kernel, fgate_bias, outnorm_scale):
        import jax, jax.numpy as jnp
        import numpy as np
        B, S, H, NH = (2, 256, 128, 4)
        DH = H // NH
        EPS = 1e-06

        def _parallel_stabilized(qh, kh, vh, ig, fg):
            log_fg = jax.nn.log_sigmoid(fg)
            cs = jnp.cumsum(log_fg, axis=2)
            ltr = jnp.tril(jnp.ones((qh.shape[2], qh.shape[2]), dtype=bool))
            log_fg_mat = jnp.where(ltr, cs - jnp.swapaxes(cs, 2, 3), -jnp.inf)
            log_D = log_fg_mat + jnp.swapaxes(ig, 2, 3)
            max_log_D = jnp.max(log_D, axis=-1, keepdims=True)
            D = jnp.exp(log_D - max_log_D)
            qk = jnp.einsum('bhsd,bhtd->bhst', qh, kh) / jnp.sqrt(jnp.float32(DH))
            C = qk * D
            normalizer = jnp.maximum(jnp.abs(jnp.sum(C, axis=-1, keepdims=True)), jnp.exp(-max_log_D))
            return jnp.einsum('bhst,bhtd->bhsd', C / (normalizer + EPS), vh)
        Bq, Sq, Hq = q.shape
        x = jnp.concatenate([q, k, v], axis=-1)
        ig = x @ igate_kernel + igate_bias
        fg = x @ fgate_kernel + fgate_bias
        ig = jnp.transpose(ig, (0, 2, 1))[..., None]
        fg = jnp.transpose(fg, (0, 2, 1))[..., None]
        qh = jnp.transpose(q.reshape(Bq, Sq, NH, DH), (0, 2, 1, 3))
        kh = jnp.transpose(k.reshape(Bq, Sq, NH, DH), (0, 2, 1, 3))
        vh = jnp.transpose(v.reshape(Bq, Sq, NH, DH), (0, 2, 1, 3))
        h = _parallel_stabilized(qh, kh, vh, ig, fg)
        mean = jnp.mean(h, axis=-1, keepdims=True)
        var = jnp.mean((h - mean) ** 2, axis=-1, keepdims=True)
        h_norm = (h - mean) * jax.lax.rsqrt(var + 1e-05)
        h_norm = h_norm * outnorm_scale.reshape(1, NH, 1, DH)
        out = jnp.transpose(h_norm, (0, 2, 1, 3)).reshape(Bq, Sq, Hq)
        return out

    def _L1_ffn_ref(x, ln_g, ln_b, rW, rb, W1, b1, W2, b2):
        import jax, jax.numpy as jnp
        import numpy as np
        E = 8
        TOP_K = 2
        LN_EPS = 1e-05

        def _layernorm(x, g, b):
            mu = jnp.mean(x, axis=-1, keepdims=True)
            var = jnp.var(x, axis=-1, keepdims=True)
            return (x - mu) * jax.lax.rsqrt(var + LN_EPS) * g + b
        z = _layernorm(x, ln_g, ln_b)
        logits = jnp.einsum('bth,he->bte', z, rW) + rb
        probs = jax.nn.softmax(logits, axis=-1)
        topv, topi = jax.lax.top_k(probs, TOP_K)
        mask = jnp.sum(jax.nn.one_hot(topi, E, dtype=probs.dtype) * topv[..., None], axis=-2)
        denom = jnp.maximum(jnp.sum(mask, axis=-1, keepdims=True), 1e-08)
        w = mask / denom
        hid = jax.nn.gelu(jnp.einsum('bth,ehf->btef', z, W1) + b1, approximate=False)
        outs = jnp.einsum('btef,efh->bteh', hid, W2) + b2
        mixed = jnp.sum(outs * w[..., None], axis=2)
        return x + mixed
    x = x + _L0_attn_ref(_layernorm(x, axis=-1), L0_attn_Wq, L0_attn_Wk, L0_attn_Wv, L0_attn_Wo)
    x = x + _L0_xattn_ref(_layernorm(x, axis=-1), ctx_1024, ctx_1024, L0_xattn_wq_w, L0_xattn_wq_b, L0_xattn_wk_w, L0_xattn_wk_b, L0_xattn_wv_w, L0_xattn_wv_b, L0_xattn_wo_w, L0_xattn_wo_b)
    x = x + _L0_ffn_ref(_layernorm(x, axis=-1), L0_ffn_router_w, L0_ffn_gate_w, L0_ffn_up_w, L0_ffn_down_w)
    x = x + _L1_attn_ref(_layernorm(x, axis=-1), L1_attn_norm_in_w, L1_attn_conv_w, L1_attn_conv_b, L1_attn_Wq, L1_attn_Wk, L1_attn_Wv, L1_attn_Wo, L1_attn_Wspike, L1_attn_Wau, L1_attn_bau, L1_attn_Wad, L1_attn_bad, L1_attn_alpha_spike, L1_attn_Wbeta, L1_attn_bbeta, L1_attn_beta_spike, L1_attn_head_norm_w, L1_attn_Wu1, L1_attn_bu1, L1_attn_Wu2, L1_attn_bu2, L1_attn_ff_norm_w, L1_attn_Wff1, L1_attn_Wff3, L1_attn_Wff2)
    x = x + _L1_xattn_ref(_layernorm(x, axis=-1), ctx_1024, ctx_1024, L1_xattn_igate_kernel, L1_xattn_igate_bias, L1_xattn_fgate_kernel, L1_xattn_fgate_bias, L1_xattn_outnorm_scale)
    x = x + _L1_ffn_ref(_layernorm(x, axis=-1), L1_ffn_ln_g, L1_ffn_ln_b, L1_ffn_rW, L1_ffn_rb, L1_ffn_W1, L1_ffn_b1, L1_ffn_W2, L1_ffn_b2)
    return x

_drawn_inputs = setup_inputs


def setup_inputs(seed=0):
    import zlib

    import numpy as np

    out = dict(_drawn_inputs(seed))
    spreads = {'L0_xattn_wq_b': (0.0, 0.384),
     'L0_xattn_wk_b': (0.0, 2.0),
     'L0_xattn_wv_b': (0.0, 0.1),
     'L0_xattn_wo_b': (0.0, 0.1),
     'L1_attn_norm_in_w': (1.0, 0.2),
     'L1_attn_conv_b': (0.0, 0.1),
     'L1_attn_bau': (0.0, 0.8),
     'L1_attn_bad': (0.0, 0.8),
     'L1_attn_alpha_spike': (0.0, 0.8),
     'L1_attn_bbeta': (0.0, 0.8),
     'L1_attn_beta_spike': (0.0, 0.777),
     'L1_attn_head_norm_w': (1.0, 0.6),
     'L1_attn_bu1': (0.0, 0.8),
     'L1_attn_bu2': (0.0, 0.8),
     'L1_attn_ff_norm_w': (1.0, 0.6),
     'L1_xattn_outnorm_scale': (1.0, 0.6),
     'L1_ffn_ln_g': (1.0, 0.6),
     'L1_ffn_ln_b': (0.0, 0.502),
     'L1_ffn_rb': (0.0, 0.624),
     'L1_ffn_b1': (0.0, 1.921),
     'L1_ffn_b2': (0.0, 1.295)}
    factors = {'L0_ffn_router_w': 5.767,
     'L0_ffn_gate_w': 5.884,
     'L0_ffn_up_w': 5.862,
     'L0_ffn_down_w': 5.773,
     'L1_attn_Wspike': 4.985,
     'L1_attn_Wau': 8.0,
     'L1_attn_Wad': 8.0,
     'L1_attn_Wbeta': 8.0,
     'L1_attn_Wu1': 8.0,
     'L1_attn_Wu2': 8.0,
     'L1_attn_Wff1': 6.815,
     'L1_attn_Wff3': 6.715,
     'L1_attn_Wff2': 6.882,
     'L1_xattn_igate_bias': 64.0,
     'L1_xattn_fgate_kernel': 15.282,
     'L1_xattn_igate_kernel': 2.951}
    for name, (base, spread) in spreads.items():
        noise = np.random.default_rng([zlib.crc32(name.encode()), seed]).standard_normal(out[name].shape)
        drawn = base * np.exp(spread * noise) if base else spread * noise
        out[name] = jnp.asarray(drawn.astype(out[name].dtype))
    for name, factor in factors.items():
        out[name] = (out[name] * factor).astype(out[name].dtype)
    return out
```

```python
from contextlib import ExitStack

import numpy as np
import concourse.bass as bass
from concourse import mybir

F32 = mybir.dt.float32
BF16 = mybir.dt.bfloat16
U8 = mybir.dt.uint8
ALU = mybir.AluOpType
ACT = mybir.ActivationFunctionType
AX = mybir.AxisListType.X

B, S, D = 64, 64, 128
GB = 8
NG = B // GB
T = GB * S
NP = GB // 2
H = 16
HP = H // 2
E0, I0 = 8, 352
I0_TILES = [(0, 128), (128, 128), (256, 96)]
HD = 8
HDP = HD // 2
E1, F1 = 8, 256
NHX, DHX = 4, 32
LEVELS = [1, 2, 4, 8, 16]
NEG = -1.0e30
LN_EPS, RMS_EPS = 1e-5, 1e-6

SMALL = [("bq", 4), ("bk", 4), ("bv", 4), ("bo", 1), ("norm_in", 1), ("conv_w", 4), ("conv_b", 1), ("bau", 1),
         ("bad", HDP), ("asp", HDP), ("bbeta", HDP), ("headw", HDP), ("bu1", 1), ("bu2", 1), ("ffw", 1),
         ("outnorm", D), ("lng", 1), ("lnb", 1), ("rb", E1), ("b1", 2 * E1), ("rank8", 8),
         ("gib", 1), ("gfb", 1), ("rw0", E0), ("rw1", E1), ("wau", 64), ("wu1", 64), ("wu2", 128), ("gates", 6 * NHX)]
SMALL_AT, _at = {}, 0
for _n, _w in SMALL:
    SMALL_AT[_n] = (_at, _w)
    _at += _w
N_SMALL = _at
CONST = ["mean", "blocksum", "ident"]


def link_of(eng, sem):
    count = [0]

    def link(ins):
        count[0] += 1
        ins.then_inc(sem, 1)
        eng.wait_ge(sem, count[0])
    return link


def build(nc, x, ctxT, ctx_tok, small, const, cmask, cmaskT, lmask, sel, w_self, w_cross, w_moe0, w_delta, w_moe1, b2, out,
          stages="ABCDEF"):
    with ExitStack() as top:
        stage = [""]

        def sb(name, shape, dt=F32, ctx=top):
            return ctx.enter_context(nc.sbuf_tensor(f"{stage[0]}{name}", shape, dt))

        bank = [top.enter_context(nc.psum_tensor(f"bank{i}", [128, 512], F32)) for i in range(8)]
        sm = sb("small_sb", [128, N_SMALL])
        cst = sb("const_sb", [128, len(CONST), 128])
        cm = sb("causal_sb", [128, 512], BF16)
        lm = sb("level_sb", [128, 6, 32], F32)
        lmi = sb("level_int_sb", [128, 6, 32], U8)
        cmT = sb("causal_t_sb", [128, 512], BF16)
        identb = sb("ident_bf", [128, 128], BF16)
        selb = sb("sel_bf", [8, 8, 128], BF16)
        self_ = sb("sel_f", [8, 8, 128])
        wA = sb("w_self_sb", [128, 4, 1024])
        wB = sb("w_cross_sb", [128, 4, 512])
        wC = sb("w_moe0_sb", [128, E0, 2 * I0 + 3 * 128])
        wD = sb("w_delta_sb", [128, 11, 512])
        wF = sb("w_moe1_sb", [128, E1, 512])
        b2s = sb("b2_sb", [8, 128])
        xg = sb("x_group", [128, T])
        cg = sb("ctx_group", [128, T])
        ctk = sb("ctx_tokens", [128, NP, NHX, DHX + 1])
        xc = sb("centred", [128, T])
        sq = sb("squared", [128, T])
        rs = sb("rstd", [128, T])
        z = sb("normed", [128, T])

        def col(name, i=0, n=1, p=128):
            at, _ = SMALL_AT[name]
            return sm[0:p, at + i:at + i + n]

        MEAN, BLOCKSUM, IDENT = (cst[:, i, :] for i in range(3))

        with ExitStack() as ctx:
            loaded = ctx.enter_context(nc.semaphore("weights_loaded"))
            with nc.Block() as block:
                @block.sync
                def _(sp):
                    loads = [(sm[:, :], small), (cst[:, :, :], const), (self_[:, :, :], sel), (b2s[:, :], b2),
                             (lm[:, :, :], lmask), (wA[:, :, :], w_self), (wB[:, :, :], w_cross),
                             (wC[:, :, :], w_moe0), (wD[:, :, :], w_delta), (wF[:, :, :], w_moe1)]
                    for dst, src in loads:
                        sp.dma_start(dst, src).then_inc(loaded, 16)
                    sp.dma_start(xc[:, :], cmask).then_inc(loaded, 16)
                    sp.dma_start(sq[:, :], cmaskT).then_inc(loaded, 16)
                    sp.wait_ge(loaded, 16 * 12)

                @block.vector
                def _(v):
                    v.wait_ge(loaded, 16 * 12)
                    v.tensor_copy(cm[:, :], xc[:, :])
                    v.tensor_copy(cmT[:, :], sq[:, :])
                    v.tensor_copy(identb[:, :], IDENT)
                    v.tensor_copy(selb[:, :, :], self_[:, :, :])
                    v.tensor_copy(lmi[:, :, :], lm[:, :, :])
            nc.all_engine_barrier(sems_to_clear=loaded)

        def run_stage(tag, names, body):
            stage[0] = tag + "_"
            with ExitStack() as ctx:
                s = {n: ctx.enter_context(nc.semaphore(f"{tag}_{n}")) for n in names.split()}
                with nc.Block() as block:
                    body(ctx, s, block)
                numbers = [x.num for x in s.values()]
                nc.all_engine_barrier(sems_to_clear=range(min(numbers), max(numbers) + 1))

        LN = "ln_mean ln_centred ln_squared ln_var ln_log ln_rstd ln_out "

        def ln_pe(pe, s, src, n=1, rms=False, mean_bank=0, var_bank=1):
            if not rms:
                pe.matmul(bank[mean_bank][:, :], MEAN, src, start=True, stop=True).then_inc(s["ln_mean"], 1)
            pe.wait_ge(s["ln_squared"], n)
            pe.matmul(bank[var_bank][:, :], MEAN, sq[:, :], start=True, stop=True).then_inc(s["ln_var"], 1)

        def ln_act(act, s, src=None, n=1, rms=False, eps=LN_EPS, var_bank=1):
            if not rms:
                act.wait_ge(s["ln_centred"], n)
            act.activation(sq[:, :], src if rms else xc[:, :], ACT.Square).then_inc(s["ln_squared"], 1)
            act.wait_ge(s["ln_var"], n)
            act.activation(rs[:, :], bank[var_bank][:, :], ACT.Sqrt, bias=eps_ap(eps)).then_inc(s["ln_log"], 1)

        eps_tiles = {}

        def eps_ap(eps):
            return eps_tiles[eps]

        def ln_dve(dve, s, src, dst, n=1, rms=False, mean_bank=0):
            if not rms:
                dve.wait_ge(s["ln_mean"], n)
                dve.tensor_tensor(xc[:, :], src, bank[mean_bank][:, :], ALU.subtract).then_inc(s["ln_centred"], 1)
            dve.wait_ge(s["ln_log"], n)
            dve.reciprocal(rs[:, :], rs[:, :]).then_inc(s["ln_rstd"], 1)
            dve.wait_ge(s["ln_rstd"], n)
            dve.tensor_tensor(dst, src if rms else xc[:, :], rs[:, :], ALU.mult).then_inc(s["ln_out"], 1)

        for eps in (LN_EPS, RMS_EPS):
            eps_tiles[eps] = sb(f"eps{len(eps_tiles)}", [128, 1])[:, :]
        with nc.Block() as block:
            @block.vector
            def _(v):
                for eps, tile in eps_tiles.items():
                    v.memset(tile, eps)

        def attention(g, cross):
            NT = 4 if cross else 8
            W = 512 if cross else 1024
            VW = 32 if cross else 64
            w = wB if cross else wA
            n_proj = 2 * NT + NP * (W // 512)
            NU = NP * 2
            scale = 1.0 / np.sqrt(8.0) if cross else 1.0 / np.sqrt(64.0)

            def heads_of(half, i):
                pair = half + 2 * i if cross else 4 * half + i
                return pair

            def body(ctx, s, block):
                qT = sb("queries", [128, NT, T], ctx=ctx)
                kT = sb("keys", [128, NT, T], ctx=ctx)
                val = sb("values", [128, NP, W], ctx=ctx)
                oT = sb("attended", [128, NT, T], ctx=ctx)
                p = sb("probs", [128, 2, 512], ctx=ctx)
                pT = sb("probs_t", [128, 2, 512], ctx=ctx)
                mx = sb("row_max", [128, 2, 8], ctx=ctx)
                sums = sb("row_sum", [128, 2, 8], ctx=ctx)

                def projection(j):
                    src = cg if cross else z
                    if j < NT:
                        return w[:, 0, j * 128:(j + 1) * 128], z[:, :], qT[:, j, :], ("bq", j)
                    if j < 2 * NT:
                        m = j - NT
                        return w[:, 1, m * 128:(m + 1) * 128], src[:, :], kT[:, m, :], ("bk", m)
                    m, c = divmod(j - 2 * NT, W // 512)
                    return src[:, m * 128:(m + 1) * 128], w[:, 2, c * 512:(c + 1) * 512], \
                        val[:, m, c * 512:(c + 1) * 512], None

                if not cross:
                    @block.sync
                    def _(sp):
                        sp.dma_start(xg[:, :], x[g, :, :]).then_inc(s["x_in"], 16)
                        sp.dma_start(cg[:, :], ctxT[g, :, :]).then_inc(s["x_in"], 16)
                        sp.dma_start(ctk[:, :, :, :], ctx_tok[g, :, :, :, :]).then_inc(s["x_in"], 16)
                        sp.wait_ge(s["x_in"], 48)

                @block.tensor
                def _(pe):
                    if not cross:
                        pe.wait_ge(s["x_in"], 48)
                    ln_pe(pe, s, xg[:, :])
                    pe.wait_ge(s["ln_out"], 1)
                    for j in range(n_proj):
                        if j >= 2:
                            pe.wait_ge(s["proj_evac_act" if j % 2 == 0 else "proj_evac_dve"], j // 2)
                        lhsT, rhs, _, _ = projection(j)
                        pe.matmul(bank[j % 2][:, :], lhsT, rhs, start=True, stop=True).then_inc(s["proj"], 1)
                    pe.wait_ge(s["proj_evac_act"], (n_proj + 1) // 2)
                    pe.wait_ge(s["proj_evac_dve"], n_proj // 2)

                    def scores(u):
                        bp, half = divmod(u, 2)
                        if u >= 2:
                            pe.wait_ge(s["shifted"], u - 1)
                        ps = bank[2 + u % 2]
                        if not cross:
                            pe.matmul(ps[:, :], identb[:, :], cm[:, :], start=True, stop=False, skip_group_check=True)
                        for i in range(4):
                            pair = heads_of(half, i)
                            for b in range(2):
                                for par in range(2):
                                    h = 2 * pair + par
                                    r0, tile, k = (32 * (h % 4), h // 4, 32) if cross else (64 * par, pair, 64)
                                    tok = (2 * bp + b) * S
                                    last = pe.matmul(ps[64 * par:64 * par + 64, i * 128 + b * 64:i * 128 + b * 64 + 64],
                                                     qT[r0:r0 + k, tile, tok:tok + S], kT[r0:r0 + k, tile, tok:tok + S],
                                                     start=cross and i == 0 and b == 0, stop=True, skip_group_check=True)
                        last.then_inc(s["scores"], 1)

                    def values(u):
                        bp, half = divmod(u, 2)
                        pe.wait_ge(s["probs"], u + 1)
                        if u >= 2:
                            pe.wait_ge(s["probs_t_evac"], u - 1)
                        for i in range(4):
                            last = pe.transpose(bank[4 + u % 2][:, i * 128:(i + 1) * 128],
                                                p[:, u % 2, i * 128:(i + 1) * 128], IDENT)
                        last.then_inc(s["probs_t"], 1)
                        pe.wait_ge(s["probs_t_evac"], u + 1)
                        if u >= 1:
                            pe.wait_ge(s["out_evac"], u)
                        for i in range(4):
                            pair = heads_of(half, i)
                            for b in range(2):
                                for par in range(2):
                                    h = 2 * pair + par
                                    r0 = 32 * (h % 4) if cross else 64 * par
                                    last = pe.matmul(bank[6 + b][r0:r0 + VW, i * 64:i * 64 + 64],
                                                     val[64 * b:64 * b + 64, bp, h * VW:(h + 1) * VW],
                                                     pT[64 * b:64 * b + 64, u % 2, i * 128 + par * 64:i * 128 + par * 64 + 64],
                                                     start=i == 0, stop=True, skip_group_check=True)
                        last.then_inc(s["attended"], 1)

                    scores(0)
                    for u in range(NU):
                        if u + 1 < NU:
                            scores(u + 1)
                        values(u)
                    pe.wait_ge(s["out_evac"], NU + cross)
                    for m in range(NT):
                        wo = w[:, 3, m * 128:(m + 1) * 128]
                        last = pe.matmul(bank[0][:, :], wo, oT[:, m, :], start=m == 0, stop=m == NT - 1)
                    last.then_inc(s["out"], 1)

                @block.scalar
                def _(act):
                    ln_act(act, s)
                    for j in range(0, n_proj, 2):
                        act.wait_ge(s["proj"], j + 1)
                        _, _, dst, bias = projection(j)
                        if cross and bias:
                            act.activation(dst, bank[0][:, :], ACT.Identity, bias=col(*bias)).then_inc(s["proj_evac_act"], 1)
                        else:
                            act.activation(dst, bank[0][:, :], ACT.Copy).then_inc(s["proj_evac_act"], 1)

                    def pt_evac(u):
                        act.wait_ge(s["probs_t"], u + 1)
                        if u >= 2:
                            act.wait_ge(s["attended"], u - 1)
                        act.activation(pT[:, u % 2, :], bank[4 + u % 2][:, :], ACT.Copy).then_inc(s["probs_t_evac"], 1)

                    for u in range(NU):
                        act.wait_ge(s["shifted"], u + 1)
                        act.activation(p[:, u % 2, :], p[:, u % 2, :], ACT.Exp, scale=float(scale)).then_inc(s["exp"], 1)
                        if u >= 1:
                            pt_evac(u - 1)
                    pt_evac(NU - 1)

                @block.vector
                def _(dve):
                    ln_dve(dve, s, xg[:, :], z[:, :])
                    for j in range(1, n_proj, 2):
                        dve.wait_ge(s["proj"], j + 1)
                        _, _, dst, bias = projection(j)
                        if cross and bias:
                            dve.tensor_scalar(dst, bank[1][:, :], col(*bias), None, ALU.add).then_inc(s["proj_evac_dve"], 1)
                        else:
                            dve.tensor_copy(dst, bank[1][:, :]).then_inc(s["proj_evac_dve"], 1)

                    def evac(u):
                        bp, half = divmod(u, 2)
                        dve.wait_ge(s["attended"], u + 1)
                        for b in range(2):
                            tok = (2 * bp + b) * S
                            if cross:
                                r = slice(64 * half, 64 * half + 64)
                                dst, src = oT[r, 0:4, tok:tok + S], bank[6 + b][r, 0:256]
                            else:
                                dst, src = oT[:, 4 * half:4 * half + 4, tok:tok + S], bank[6 + b][:, 0:256]
                            last = dve.tensor_copy(dst, src.rearrange("p (i t) -> p i t", t=S))
                        last.then_inc(s["out_evac"], 1)

                    for u in range(NU):
                        i = u % 2
                        ps = bank[2 + i][:, :].rearrange("p (h k) -> p h k", k=S)
                        pr = p[:, i, :].rearrange("p (h k) -> p h k", k=S)
                        dve.wait_ge(s["scores"], u + 1)
                        dve.tensor_reduce(mx[:, i, :], ps, AX, ALU.max).then_inc(s["max"], 1)
                        dve.wait_ge(s["max"], u + 1)
                        if u >= 2:
                            dve.wait_ge(s["probs_t"], u - 1)
                        dve.tensor_tensor(pr, ps, mx[:, i, :].unsqueeze(2).to_broadcast([128, 8, S]), ALU.subtract)\
                            .then_inc(s["shifted"], 1)
                        if u >= 1:
                            evac(u - 1)
                        dve.wait_ge(s["exp"], u + 1)
                        dve.tensor_reduce(sums[:, i, :], pr, AX, ALU.add).then_inc(s["sum"], 1)
                        dve.wait_ge(s["sum"], u + 1)
                        dve.reciprocal(sums[:, i, :], sums[:, i, :]).then_inc(s["rsum"], 1)
                    evac(NU - 1)
                    if cross:
                        dve.wait_ge(s["out_evac"], NU)
                        for m in range(NT):
                            last = dve.tensor_scalar(oT[:, m, :], oT[:, m, :], col("bv", m), None, ALU.add)
                        last.then_inc(s["out_evac"], 1)
                    dve.wait_ge(s["out"], 1)
                    if cross:
                        dve.scalar_tensor_tensor(xg[:, :], bank[0][:, :], col("bo"), xg[:, :], ALU.add, ALU.add)
                    else:
                        dve.tensor_tensor(xg[:, :], xg[:, :], bank[0][:, :], ALU.add)

                @block.gpsimd
                def _(pool):
                    for u in range(NU):
                        i = u % 2
                        pr = p[:, i, :].rearrange("p (h k) -> p h k", k=S)
                        pool.wait_ge(s["rsum"], u + 1)
                        pool.tensor_tensor(pr, pr, sums[:, i, :].unsqueeze(2).to_broadcast([128, 8, S]), ALU.mult)\
                            .then_inc(s["probs"], 1)

            run_stage("cross" if cross else "self", LN + "x_in proj proj_evac_act proj_evac_dve scores max shifted exp sum rsum probs probs_t "
                           "probs_t_evac attended out_evac out", body)

        def moe0(g):
            NT = len(I0_TILES)

            def body(ctx, s, block):
                oh = sb("one_hot", [128, 4, E0], ctx=ctx)
                rank = sb("rank", [128, 4, E0], ctx=ctx)
                m1 = sb("best", [128, 4], ctx=ctx)
                ohT = sb("one_hot_t", [E0, T], BF16, ctx=ctx)
                ze = sb("z_expert", [128, 2, T], ctx=ctx)
                sg = sb("silu_gate", [128, 2, T], ctx=ctx)
                h = sb("hidden", [128, 2, T], ctx=ctx)
                steps = [(e, i) for e in range(E0) for i in range(NT)]

                @block.tensor
                def _(pe):
                    ln_pe(pe, s, xg[:, :])
                    pe.wait_ge(s["ln_out"], 1)
                    for i in range(4):
                        last = pe.matmul(bank[2][:, i * E0:(i + 1) * E0], z[:, i * 128:(i + 1) * 128], col("rw0", 0, E0),
                                         start=True, stop=True, skip_group_check=True)
                    last.then_inc(s["logits"], 1)
                    pe.wait_ge(s["one_hot"], 1)
                    for i in range(4):
                        last = pe.transpose(bank[3][0:E0, i * 128:(i + 1) * 128], oh[:, i, :], IDENT)
                    last.then_inc(s["one_hot_ps"], 1)
                    pe.wait_ge(s["one_hot_t"], 1)

                    def down(k):
                        e, i = steps[k]
                        n = I0_TILES[i][1]
                        pe.wait_ge(s["hidden"], k + 1)
                        pe.matmul(bank[7][:, :], wC[0:n, e, 2 * I0 + i * 128:2 * I0 + (i + 1) * 128], h[0:n, k % 2, :],
                                  start=k == 0, stop=k == len(steps) - 1).then_inc(s["down"], 1)

                    for k, (e, i) in enumerate(steps):
                        if i == 0:
                            if e >= 1:
                                pe.wait_ge(s["masked"], e)
                            pe.matmul(bank[2][:, :], selb[:, e, :], ohT[:, :], start=True, stop=True).then_inc(s["bcast"], 1)
                            pe.wait_ge(s["masked"], e + 1)
                        if k >= 2:
                            pe.wait_ge(s["hidden"], k - 1)
                        at, n = I0_TILES[i]
                        pe.matmul(bank[3 + k % 2][0:n, :], wC[:, e, at:at + n], ze[:, e % 2, :], start=True, stop=True)\
                            .then_inc(s["gate"], 1)
                        pe.matmul(bank[5 + k % 2][0:n, :], wC[:, e, I0 + at:I0 + at + n], ze[:, e % 2, :], start=True,
                                  stop=True).then_inc(s["up"], 1)
                        if k >= 1:
                            down(k - 1)
                    down(len(steps) - 1)

                @block.scalar
                def _(act):
                    ln_act(act, s)
                    for k, (e, i) in enumerate(steps):
                        n = I0_TILES[i][1]
                        act.wait_ge(s["gate"], k + 1)
                        if k >= 2:
                            act.wait_ge(s["hidden"], k - 1)
                        act.activation(sg[0:n, k % 2, :], bank[3 + k % 2][0:n, :], ACT.Silu).then_inc(s["silu"], 1)

                @block.vector
                def _(dve):
                    link = link_of(dve, s["dve"])
                    ln_dve(dve, s, xg[:, :], z[:, :])
                    lg = bank[2][:, 0:4 * E0].rearrange("p (i e) -> p i e", e=E0)
                    dve.wait_ge(s["logits"], 1)
                    link(dve.tensor_reduce(m1[:, :], lg, AX, ALU.max))
                    link(dve.tensor_tensor(oh[:, :, :], lg, m1[:, :].unsqueeze(2).to_broadcast([128, 4, E0]), ALU.is_equal))
                    link(dve.tensor_tensor(rank[:, :, :], oh[:, :, :],
                                           col("rank8", 0, 8).unsqueeze(1).to_broadcast([128, 4, E0]), ALU.mult))
                    link(dve.tensor_reduce(m1[:, :], rank[:, :, :], AX, ALU.max))
                    dve.tensor_tensor(oh[:, :, :], rank[:, :, :], m1[:, :].unsqueeze(2).to_broadcast([128, 4, E0]),
                                      ALU.is_equal).then_inc(s["one_hot"], 1)
                    dve.wait_ge(s["one_hot_ps"], 1)
                    dve.tensor_copy(ohT[:, :], bank[3][0:E0, :]).then_inc(s["one_hot_t"], 1)

                    def mask(e):
                        dve.wait_ge(s["bcast"], e + 1)
                        if e >= 2:
                            dve.wait_ge(s["up"], NT * (e - 1))
                        dve.tensor_tensor(ze[:, e % 2, :], z[:, :], bank[2][:, :], ALU.mult).then_inc(s["masked"], 1)

                    for k, (e, i) in enumerate(steps):
                        n = I0_TILES[i][1]
                        if i == 0:
                            mask(e)
                        dve.wait_ge(s["silu"], k + 1)
                        dve.wait_ge(s["up"], k + 1)
                        if k >= 2:
                            dve.wait_ge(s["down"], k - 1)
                        dve.tensor_tensor(h[0:n, k % 2, :], sg[0:n, k % 2, :], bank[5 + k % 2][0:n, :], ALU.mult)\
                            .then_inc(s["hidden"], 1)
                    dve.wait_ge(s["down"], len(steps))
                    dve.tensor_tensor(xg[:, :], xg[:, :], bank[7][:, :], ALU.add)

            run_stage("moe0", LN + "logits one_hot one_hot_ps one_hot_t bcast masked gate up silu hidden down dve", body)

        def moe1(g):
            def body(ctx, s, block):
                z2 = sb("z2", [128, T], ctx=ctx)
                p = sb("gate_probs", [128, 4, E1], ctx=ctx)
                rank = sb("rank", [128, 4, E1], ctx=ctx)
                oh = sb("one_hot", [128, 4, E1], ctx=ctx)
                keep = sb("kept", [128, 4, E1], ctx=ctx)
                m1 = sb("best", [128, 4], ctx=ctx)
                wT = sb("weights_t", [E1, T], ctx=ctx)
                wbc = sb("weight_bc", [128, 2, T], ctx=ctx)
                hid = sb("hid", [128, 2, T], ctx=ctx)
                h = sb("hidden", [128, 2, T], ctx=ctx)
                steps = [(e, i) for e in range(E1) for i in range(2)]

                def bc(t):
                    return t[:, :].unsqueeze(2).to_broadcast([128, 4, E1])

                @block.tensor
                def _(pe):
                    ln_pe(pe, s, xg[:, :])
                    pe.wait_ge(s["ln_out"], 1)
                    ln_pe(pe, s, z[:, :], n=2)
                    pe.wait_ge(s["z2"], 1)
                    for i in range(4):
                        last = pe.matmul(bank[2][:, i * E1:(i + 1) * E1], z2[:, i * 128:(i + 1) * 128], col("rw1", 0, E1),
                                         start=True, stop=True, skip_group_check=True)
                    last.then_inc(s["logits"], 1)
                    pe.wait_ge(s["weights"], 1)
                    for i in range(4):
                        last = pe.transpose(bank[3][0:E1, i * 128:(i + 1) * 128], p[:, i, :], IDENT)
                    last.then_inc(s["weights_ps"], 1)
                    pe.wait_ge(s["weights_t"], 1)
                    pe.matmul(bank[7][:, :], b2s[:, :], wT[:, :], start=True, stop=False)

                    def down(k):
                        e, i = steps[k]
                        pe.wait_ge(s["hidden"], k + 1)
                        pe.matmul(bank[7][:, :], wF[:, e, 256 + i * 128:256 + (i + 1) * 128], h[:, k % 2, :],
                                  start=False, stop=k == len(steps) - 1).then_inc(s["down"], 1)

                    for k, (e, i) in enumerate(steps):
                        if i == 0:
                            if e >= 2:
                                pe.wait_ge(s["hidden"], 2 * (e - 1))
                            pe.matmul(bank[2 + e % 2][:, :], self_[:, e, :], wT[:, :], start=True, stop=True)\
                                .then_inc(s["bcast"], 1)
                        if k >= 2:
                            pe.wait_ge(s["gelu"], k - 1)
                        pe.matmul(bank[4 + k % 2][:, :], wF[:, e, i * 128:(i + 1) * 128], z2[:, :], start=True, stop=True)\
                            .then_inc(s["up"], 1)
                        if k >= 1:
                            down(k - 1)
                    down(len(steps) - 1)

                @block.scalar
                def _(act):
                    ln_act(act, s)
                    ln_act(act, s, n=2)
                    act.wait_ge(s["shifted"], 1)
                    act.activation(p[:, :, :], p[:, :, :], ACT.Exp).then_inc(s["exp"], 1)
                    for k, (e, i) in enumerate(steps):
                        act.wait_ge(s["up"], k + 1)
                        if k >= 2:
                            act.wait_ge(s["hidden"], k - 1)
                        act.activation(hid[:, k % 2, :], bank[4 + k % 2][:, :], ACT.Gelu, bias=col("b1", 2 * e + i))\
                            .then_inc(s["gelu"], 1)

                @block.vector
                def _(dve):
                    link = link_of(dve, s["dve"])
                    ln_dve(dve, s, xg[:, :], z[:, :])
                    dve.wait_ge(s["ln_out"], 1)
                    ln_dve(dve, s, z[:, :], z2[:, :], n=2)
                    dve.wait_ge(s["ln_out"], 2)
                    dve.tensor_scalar(z2[:, :], z2[:, :], col("lng"), col("lnb"), ALU.mult, ALU.add).then_inc(s["z2"], 1)
                    dve.wait_ge(s["logits"], 1)
                    lg = bank[2][:, 0:4 * E1].rearrange("p (i e) -> p i e", e=E1)
                    link(dve.tensor_tensor(p[:, :, :], lg, col("rb", 0, E1).unsqueeze(1).to_broadcast([128, 4, E1]), ALU.add))
                    link(dve.tensor_reduce(m1[:, :], p[:, :, :], AX, ALU.max))
                    dve.tensor_tensor(p[:, :, :], p[:, :, :], bc(m1), ALU.subtract).then_inc(s["shifted"], 1)
                    dve.wait_ge(s["exp"], 1)
                    link(dve.tensor_reduce(m1[:, :], p[:, :, :], AX, ALU.add))
                    link(dve.reciprocal(m1[:, :], m1[:, :]))
                    link(dve.tensor_tensor(p[:, :, :], p[:, :, :], bc(m1), ALU.mult))
                    link(dve.tensor_copy(keep[:, :, :], p[:, :, :]))
                    for r in range(2):
                        link(dve.tensor_reduce(m1[:, :], keep[:, :, :], AX, ALU.max))
                        link(dve.tensor_tensor(oh[:, :, :], keep[:, :, :], bc(m1), ALU.is_equal))
                        link(dve.tensor_tensor(rank[:, :, :], oh[:, :, :],
                                               col("rank8", 0, 8).unsqueeze(1).to_broadcast([128, 4, E1]), ALU.mult))
                        link(dve.tensor_reduce(m1[:, :], rank[:, :, :], AX, ALU.max))
                        link(dve.tensor_tensor(oh[:, :, :], rank[:, :, :], bc(m1), ALU.is_equal))
                        link(dve.scalar_tensor_tensor(keep[:, :, :], oh[:, :, :], -2.0, keep[:, :, :], ALU.mult, ALU.add))
                    link(dve.scalar_tensor_tensor(p[:, :, :], keep[:, :, :], 0.0, p[:, :, :], ALU.is_lt, ALU.mult))
                    link(dve.tensor_reduce(m1[:, :], p[:, :, :], AX, ALU.add))
                    link(dve.tensor_scalar(m1[:, :], m1[:, :], 1e-8, None, ALU.max))
                    link(dve.reciprocal(m1[:, :], m1[:, :]))
                    dve.tensor_tensor(p[:, :, :], p[:, :, :], bc(m1), ALU.mult).then_inc(s["weights"], 1)
                    dve.wait_ge(s["weights_ps"], 1)
                    dve.tensor_copy(wT[:, :], bank[3][0:E1, :]).then_inc(s["weights_t"], 1)
                    for k, (e, i) in enumerate(steps):
                        dve.wait_ge(s["bcast"], e + 1)
                        dve.wait_ge(s["gelu"], k + 1)
                        if k >= 2:
                            dve.wait_ge(s["down"], k - 1)
                        dve.tensor_tensor(h[:, k % 2, :], hid[:, k % 2, :], bank[2 + e % 2][:, :], ALU.mult)\
                            .then_inc(s["hidden"], 1)
                    dve.wait_ge(s["down"], len(steps))
                    link(dve.tensor_tensor(xg[:, :], xg[:, :], bank[7][:, :], ALU.add))
                    dve.tensor_tensor(xg[:, :], xg[:, :], z[:, :], ALU.add).then_inc(s["x_out"], 1)

            run_stage("moe1", LN + "z2 logits shifted exp weights weights_ps weights_t bcast up gelu hidden down dve x_out", body)

        def delta(g):
            U_ = GB * HDP
            PB = 8

            def body(ctx, s, block):
                hc = sb("conv_in", [128, GB, S + 3], ctx=ctx)
                h = sb("conv_out", [128, T], ctx=ctx)
                au = sb("alpha_low", [64, T], ctx=ctx)
                tmp = sb("tmp", [128, 2, T], ctx=ctx)
                nb = sb("norms", [128, 2, T], ctx=ctx)
                mem = sb("membrane", [128, HDP, GB], ctx=ctx)
                spike = sb("spike", [128, HDP, T], ctx=ctx)
                drive = sb("drive", [128, HDP, T], ctx=ctx)
                al = sb("decays", [128, HDP, T], ctx=ctx)
                kq = sb("scaled_kq", [128, 2, HDP, T], ctx=ctx)
                kr = sb("scaled_beta_k", [128, HDP, T], ctx=ctx)
                aT = sb("level_a_t", [128, U_, 32], ctx=ctx)
                X = sb("inverse", [128, U_, 32], ctx=ctx)
                XT = sb("inverse_t", [128, U_, 32], ctx=ctx)
                W = sb("a_times_inverse", [128, U_, 32], ctx=ctx)
                pc = sb("p_t_blocks", [128, U_, 32], ctx=ctx)
                oT = spike
                U = drive[:, :, :].rearrange("p a (b v) -> p (a b) v", v=64)
                R = al[:, :, :].rearrange("p a (b v) -> p (a b) v", v=64)
                V = kq[:, 0, :, :].rearrange("p a (b v) -> p (a b) v", v=64)
                PT = kr[:, :, :].rearrange("p a (b v) -> p (a b) v", v=64)

                def wide(t, bk, n=32):
                    return t[:, bk * PB:(bk + 1) * PB, :]

                def level(l):
                    return lm[:, l, :].unsqueeze(1).to_broadcast([128, PB, 32])

                def units():
                    for u in range(U_):
                        yield (u,) + divmod(u, HDP)

                @block.tensor
                def _(pe):
                    ln_pe(pe, s, xg[:, :])
                    pe.wait_ge(s["ln_out"], 1)
                    ln_pe(pe, s, z[:, :], n=2, rms=True)
                    pe.wait_ge(s["h"], 1)
                    pe.matmul(bank[6][0:64, :], col("wau", 0, 64), h[:, :], start=True, stop=True).then_inc(s["au_ps"], 1)
                    for j in range(16):
                        kind, m = divmod(j, 4)
                        if j >= 4:
                            pe.wait_ge(s["proj_read"], j - 3)
                        if kind == 3:
                            pe.wait_ge(s["au"], 1)
                            lhsT, rhs = wD[0:64, 4, m * 128:(m + 1) * 128], au[:, :]
                        else:
                            lhsT, rhs = wD[:, (3, 0, 1)[kind], m * 128:(m + 1) * 128], h[:, :]
                        pe.matmul(bank[j % 4][:, :], lhsT, rhs, start=True, stop=True).then_inc(s["proj"], 1)
                    for n in range(8):
                        pe.wait_ge(s["squared"], n + 1)
                        if n >= 2:
                            pe.wait_ge(s["norm"], n - 1)
                        pe.matmul(bank[4 + n % 2][:, :], BLOCKSUM, tmp[:, n % 2, :], start=True, stop=True)\
                            .then_inc(s["norm_ps"], 1)
                    pe.wait_ge(s["norm"], 8)
                    pe.wait_ge(s["spikes"], 1)
                    for j in range(HDP):
                        if j >= 2:
                            pe.wait_ge(s["kr"], j - 1)
                        pe.matmul(bank[4 + j % 2][:, :], BLOCKSUM, spike[:, j, :], start=True, stop=True)\
                            .then_inc(s["count"], 1)
                        pe.matmul(bank[6 + j % 2][:, :], wD[:, 5, j * 128:(j + 1) * 128], h[:, :], start=True, stop=False)
                        pe.matmul(bank[6 + j % 2][:, :], wD[:, 6, j * 128:(j + 1) * 128], spike[:, j, :], start=False,
                                  stop=True).then_inc(s["beta_ps"], 1)
                    pe.wait_ge(s["kr"], HDP)
                    for u, b, hp in units():
                        for q in range(4):
                            r, t0 = slice(64 * (q // 2), 64 * (q // 2) + 64), b * S + 32 * (q % 2)
                            last = pe.matmul(bank[u // 16][32 * q:32 * q + 32, (u % 16) * 32:(u % 16) * 32 + 32],
                                             kr[r, hp, t0:t0 + 32], kq[r, 1, hp, t0:t0 + 32], start=u % 16 == 0, stop=True,
                                             skip_group_check=True)
                    last.then_inc(s["diag_ps"], 1)

                    def products(l):
                        pe.wait_ge(s["scaled"], l + 1)
                        if l == 0:
                            pe.wait_ge(s["diag"], 1)
                        else:
                            pe.wait_ge(s["masked"], l)
                        for u, b, hp in units():
                            for q in range(4):
                                r, t0 = slice(64 * (q // 2), 64 * (q // 2) + 64), b * S + 32 * (q % 2)
                                last = pe.matmul(bank[u // PB][32 * q:32 * q + 32, (u % PB) * 64:(u % PB) * 64 + 64],
                                                 kr[r, hp, t0:t0 + 32], kq[r, :, hp, t0:t0 + 32], start=u % PB == 0,
                                                 stop=True, skip_group_check=True)
                        last.then_inc(s["products"], 1)

                    def blockwise(first_bank, lhsT, rhs, sem):
                        for u in range(U_):
                            for q in range(4):
                                r = slice(32 * q, 32 * q + 32)
                                last = pe.matmul(bank[first_bank + u // 16][r, (u % 16) * 32:(u % 16) * 32 + 32],
                                                 lhsT[r, u, :], rhs[r, u, :], start=u % 16 == 0, stop=True,
                                                 skip_group_check=True)
                        last.then_inc(s[sem], 1)

                    products(0)
                    for l in range(1, len(LEVELS)):
                        products(l)
                        pe.wait_ge(s["masked"], l + 1)
                        pe.wait_ge(s["inverse"], l)
                        blockwise(4, aT, X, "w_ps")
                        pe.wait_ge(s["w"], l)
                        blockwise(6, XT, W, "xw_ps")
                    pe.wait_ge(s["scaled"], len(LEVELS) + 1)
                    pe.wait_ge(s["masked"], len(LEVELS))
                    for u, b, hp in units():
                        for par in range(2):
                            r = slice(64 * par, 64 * par + 64)
                            last = pe.matmul(bank[u // PB][64 * par:64 * par + 32, (u % PB) * 64:(u % PB) * 64 + 64],
                                             kr[r, hp, b * S:b * S + 32], kq[r, :, hp, b * S + 32:b * S + 64],
                                             start=u % PB == 0, stop=True, skip_group_check=True)
                    last.then_inc(s["join_ps"], 1)
                    pe.wait_ge(s["inverse"], len(LEVELS))
                    for b in range(GB):
                        for par in range(2):
                            last = pe.matmul(bank[4 + b // 2][64 * par:64 * par + 64, (b % 2) * 256:(b % 2) * 256 + 256],
                                             h[:, b * S:(b + 1) * S], wD[:, 2, par * 256:(par + 1) * 256],
                                             start=b % 2 == 0, stop=True, skip_group_check=True)
                    last.then_inc(s["v_ps"], 1)
                    pe.wait_ge(s["v"], 1)
                    pe.wait_ge(s["joined"], 1)
                    for u in range(U_):
                        for q in range(4):
                            r = slice(32 * q, 32 * q + 32)
                            last = pe.matmul(bank[u // PB][r, (u % PB) * 64:(u % PB) * 64 + 64], XT[r, u, :], V[r, u, :],
                                             start=u % PB == 0, stop=True, skip_group_check=True)
                    last.then_inc(s["y_ps"], 1)
                    pe.wait_ge(s["y"], 1)
                    for u in range(U_):
                        for par in range(2):
                            r, r2 = slice(64 * par, 64 * par + 32), slice(64 * par + 32, 64 * par + 64)
                            last = pe.matmul(bank[4 + u // PB][r2, (u % PB) * 64:(u % PB) * 64 + 64], aT[r, u, :], U[r, u, :],
                                             start=u % PB == 0, stop=True, skip_group_check=True)
                    last.then_inc(s["r_ps"], 1)
                    pe.wait_ge(s["r"], 1)
                    for u in range(U_):
                        for par in range(2):
                            r2 = slice(64 * par + 32, 64 * par + 64)
                            last = pe.matmul(bank[u // PB][r2, (u % PB) * 64:(u % PB) * 64 + 64], XT[r2, u, :], R[r2, u, :],
                                             start=u % PB == 0, stop=True, skip_group_check=True)
                    last.then_inc(s["u2_ps"], 1)
                    pe.wait_ge(s["u"], 1)
                    for u, b, hp in units():
                        for par in range(2):
                            r = slice(64 * par, 64 * par + 64)
                            last = pe.matmul(bank[4 + hp][r, b * S:(b + 1) * S], U[r, u, :], PT[r, u, :], start=b == 0,
                                             stop=True, skip_group_check=True)
                    last.then_inc(s["o_ps"], 1)
                    for n in range(HDP):
                        pe.wait_ge(s["o_squared"], n + 1)
                        if n >= 2:
                            pe.wait_ge(s["o_norm"], n - 1)
                        pe.matmul(bank[n % 2][:, :], BLOCKSUM, tmp[:, n % 2, :], start=True, stop=True)\
                            .then_inc(s["o_norm_ps"], 1)
                    pe.matmul(bank[3][0:64, :], col("wu1", 0, 64), z[:, :], start=True, stop=True).then_inc(s["g1_ps"], 1)
                    pe.wait_ge(s["o"], HDP)
                    for n in range(HDP):
                        last = pe.matmul(bank[2][:, :], wD[:, 7, n * 128:(n + 1) * 128], oT[:, n, :], start=n == 0,
                                         stop=n == HDP - 1)
                    last.then_inc(s["wo_ps"], 1)
                    pe.wait_ge(s["g1"], 1)
                    pe.matmul(bank[4][:, :], col("wu2", 0, 128, p=64), au[:, :], start=True, stop=True).then_inc(s["g2_ps"], 1)
                    pe.wait_ge(s["y2"], 1)
                    ln_pe(pe, s, h[:, :], n=3, rms=True)
                    pe.wait_ge(s["zz"], 1)
                    for n in range(4):
                        if n >= 2:
                            pe.wait_ge(s["ff"], n - 1)
                        pe.matmul(bank[2 + n % 2][:, :], wD[:, 8, n * 128:(n + 1) * 128], z[:, :], start=True, stop=True)
                        pe.matmul(bank[4 + n % 2][:, :], wD[:, 9, n * 128:(n + 1) * 128], z[:, :], start=True, stop=True)\
                            .then_inc(s["ff_ps"], 1)
                    for n in range(4):
                        pe.wait_ge(s["ff"], n + 1)
                        last = pe.matmul(bank[6][:, :], wD[:, 10, n * 128:(n + 1) * 128], drive[:, n, :], start=n == 0,
                                         stop=n == 3)
                    last.then_inc(s["down"], 1)

                @block.scalar
                def _(act):
                    ln_act(act, s)
                    act.wait_ge(s["ln_out"], 1)
                    ln_act(act, s, src=z[:, :], n=2, rms=True, eps=RMS_EPS)
                    act.wait_ge(s["conv"], 1)
                    act.activation(h[:, :], tmp[:, 0, :], ACT.Silu, bias=col("conv_b")).then_inc(s["h"], 1)
                    act.wait_ge(s["au_ps"], 1)
                    act.activation(au[:, :], bank[6][0:64, :], ACT.Silu, bias=col("bau", p=64)).then_inc(s["au"], 1)

                    def root(n):
                        act.wait_ge(s["norm_ps"], n + 1)
                        if n >= 2:
                            act.wait_ge(s["normed"], n - 1)
                        act.activation(nb[:, n % 2, :], bank[4 + n % 2][:, :], ACT.Sqrt).then_inc(s["norm"], 1)
                    for n in range(8):
                        act.wait_ge(s["proj_read"], 4 + n + 1)
                        if n >= 2:
                            act.wait_ge(s["norm_ps"], n - 1)
                        if n == 0:
                            act.wait_ge(s["h"], 1)
                        act.activation(tmp[:, n % 2, :], kq[:, (n // 4 + 1) % 2, n % 4, :], ACT.Square).then_inc(s["squared"], 1)
                        if n >= 1:
                            root(n - 1)
                    root(7)
                    for j in range(HDP):
                        act.wait_ge(s["alpha_pre"], j + 1)
                        act.activation(al[:, j, :], al[:, j, :], ACT.Sigmoid, bias=col("bad", j)).then_inc(s["alpha"], 1)
                        act.wait_ge(s["beta_ps"], j + 1)
                        if j >= 2:
                            act.wait_ge(s["kr"], j - 1)
                        act.activation(nb[:, j % 2, :], bank[6 + j % 2][:, :], ACT.Sigmoid, bias=col("bbeta", j))\
                            .then_inc(s["beta"], 1)
                    for l in range(1, len(LEVELS)):
                        act.wait_ge(s["w_ps"], l)
                        for i in range(2):
                            last = act.activation(W[:, 16 * i:16 * i + 16, :],
                                                  bank[4 + i][:, :].rearrange("p (u n) -> p u n", n=32), ACT.Copy)
                        last.then_inc(s["w"], 1)
                    act.wait_ge(s["join_ps"], 1)
                    act.wait_ge(s["masked"], len(LEVELS))
                    act.wait_ge(s["zeros"], 1)
                    for q in range(4):
                        r = slice(32 * q, 32 * q + 32)
                        last = act.activation(PT[r, :, 32 * (q % 2):32 * (q % 2) + 32], pc[r, :, :], ACT.Copy)
                        if q % 2 == 0:
                            for bk in range(4):
                                last = act.activation(
                                    PT[r, bk * PB:(bk + 1) * PB, 32:64],
                                    bank[bk][r, :].rearrange("p (u n) -> p u n", n=64)[:, :, 32:64], ACT.Copy)
                    last.then_inc(s["p_t"], 1)
                    act.wait_ge(s["v_ps"], 1)
                    for bk in range(4):
                        last = act.activation(wide(V, bk), bank[4 + bk][:, :].rearrange("p (u n) -> p u n", n=64), ACT.Copy)
                    last.then_inc(s["v"], 1)
                    act.wait_ge(s["r_ps"], 1)
                    for bk in range(4):
                        for par in range(2):
                            r2 = slice(64 * par + 32, 64 * par + 64)
                            last = act.activation(R[r2, bk * PB:(bk + 1) * PB, :],
                                                  bank[4 + bk][r2, :].rearrange("p (u n) -> p u n", n=64), ACT.Copy)
                    last.then_inc(s["r"], 1)

                    act.wait_ge(s["o_ps"], 1)

                    def o_root(n):
                        act.wait_ge(s["o_norm_ps"], n + 1)
                        if n >= 2:
                            act.wait_ge(s["o"], n - 1)
                        act.activation(nb[:, n % 2, :], bank[n % 2][:, :], ACT.Sqrt, bias=eps_ap(RMS_EPS), scale=1.0 / 64)\
                            .then_inc(s["o_norm"], 1)
                    for n in range(HDP):
                        if n >= 2:
                            act.wait_ge(s["o_norm_ps"], n - 1)
                        act.activation(tmp[:, n % 2, :], bank[4 + n][:, :], ACT.Square).then_inc(s["o_squared"], 1)
                        if n >= 1:
                            o_root(n - 1)
                    o_root(HDP - 1)
                    act.wait_ge(s["g1_ps"], 1)
                    act.activation(au[:, :], bank[3][0:64, :], ACT.Silu, bias=col("bu1", p=64)).then_inc(s["g1"], 1)
                    act.wait_ge(s["g2_ps"], 1)
                    act.activation(tmp[:, 0, :], bank[4][:, :], ACT.Sigmoid, bias=col("bu2")).then_inc(s["g2"], 1)
                    act.wait_ge(s["y2"], 1)
                    ln_act(act, s, src=h[:, :], n=3, rms=True, eps=RMS_EPS)
                    for n in range(4):
                        act.wait_ge(s["ff_ps"], n + 1)
                        if n >= 2:
                            act.wait_ge(s["ff"], n - 1)
                        act.activation(tmp[:, n % 2, :], bank[2 + n % 2][:, :], ACT.Silu).then_inc(s["ff_silu"], 1)

                @block.gpsimd
                def _(pool):
                    pool.memset(hc[:, :, 0:3], 0.0).then_inc(s["pad"], 1)
                    pool.wait_ge(s["join_ps"], 1)
                    for par in range(2):
                        last = pool.memset(PT[64 * par + 32:64 * par + 64, :, 0:32], 0.0)
                    last.then_inc(s["zeros"], 1)

                @block.vector
                def _(dve):
                    link = link_of(dve, s["dve"])
                    ln_dve(dve, s, xg[:, :], z[:, :])
                    dve.wait_ge(s["ln_log"], 2)
                    link(dve.reciprocal(rs[:, :], rs[:, :]))
                    dve.wait_ge(s["ln_out"], 1)
                    dve.wait_ge(s["pad"], 1)

                    def tok(t):
                        return t.rearrange("p (b t) -> p b t", t=S)
                    link(dve.scalar_tensor_tensor(hc[:, :, 3:3 + S], tok(z[:, :]), col("norm_in"), tok(rs[:, :]), ALU.mult,
                                                  ALU.mult))
                    cv = tok(tmp[:, 0, :])
                    link(dve.tensor_scalar(cv, hc[:, :, 0:S], col("conv_w", 0), None, ALU.mult))
                    for i in range(1, 4):
                        last = dve.scalar_tensor_tensor(cv, hc[:, :, i:i + S], col("conv_w", i), cv, ALU.mult, ALU.add)
                        if i < 3:
                            link(last)
                    last.then_inc(s["conv"], 1)
                    for j in range(16):
                        kind, m = divmod(j, 4)
                        dst = (drive[:, m, :], kq[:, 1, m, :], kq[:, 0, m, :], al[:, m, :])[kind]
                        dve.wait_ge(s["proj"], j + 1)
                        dve.tensor_copy(dst, bank[j % 4][:, :]).then_inc(s["proj_read"], 1)
                    for n in range(8):
                        dve.wait_ge(s["norm"], n + 1)
                        link(dve.tensor_scalar(nb[:, n % 2, :], nb[:, n % 2, :], 1e-6, None, ALU.add))
                        link(dve.reciprocal(nb[:, n % 2, :], nb[:, n % 2, :]))
                        x_ = kq[:, (n // 4 + 1) % 2, n % 4, :]
                        dve.tensor_tensor(x_, x_, nb[:, n % 2, :], ALU.mult).then_inc(s["normed"], 1)
                    dve.wait_ge(s["proj_read"], 16)
                    dr, sp_ = (t[:, :, :].rearrange("p h (b t) -> p h b t", t=S) for t in (drive, spike))
                    for t in range(S):
                        if t == 0:
                            link(dve.tensor_copy(mem[:, :, :], dr[:, :, :, 0]))
                        else:
                            link(dve.scalar_tensor_tensor(mem[:, :, :], mem[:, :, :], 0.9, dr[:, :, :, t], ALU.mult, ALU.add))
                        link(dve.tensor_scalar(sp_[:, :, :, t], mem[:, :, :], 0.5, None, ALU.is_gt))
                        last = dve.scalar_tensor_tensor(mem[:, :, :], sp_[:, :, :, t], -0.5, mem[:, :, :], ALU.mult, ALU.add)
                        if t < S - 1:
                            link(last)
                    last.then_inc(s["spikes"], 1)
                    dve.wait_ge(s["spikes"], 1)
                    for j in range(HDP):
                        dve.scalar_tensor_tensor(al[:, j, :], spike[:, j, :], col("asp", j), al[:, j, :], ALU.mult, ALU.add)\
                            .then_inc(s["alpha_pre"], 1)
                    dve.wait_ge(s["normed"], 8)
                    for j in range(HDP):
                        dve.wait_ge(s["count"], j + 1)
                        dve.wait_ge(s["alpha"], j + 1)
                        dve.scalar_tensor_tensor(al[:, j, :], bank[4 + j % 2][:, :], 0.0, al[:, j, :], ALU.is_equal, ALU.max)
                        dve.wait_ge(s["beta"], j + 1)
                        link(dve.scalar_tensor_tensor(nb[:, j % 2, :], bank[4 + j % 2][:, :], 0.0, nb[:, j % 2, :], ALU.is_gt,
                                                      ALU.mult))
                        dve.tensor_tensor(kr[:, j, :], kq[:, 0, j, :], nb[:, j % 2, :], ALU.mult).then_inc(s["kr"], 1)
                    dve.wait_ge(s["diag_ps"], 1)
                    for i in range(2):
                        last = dve.tensor_tensor(pc[:, 16 * i:16 * i + 16, :],
                                                 bank[i][:, :].rearrange("p (u n) -> p u n", n=32),
                                                 lm[:, 5, :].unsqueeze(1).to_broadcast([128, 16, 32]), ALU.mult)
                    last.then_inc(s["diag"], 1)
                    dve.wait_ge(s["kr"], HDP)
                    flat = lambda t: t.rearrange("p h t -> p (h t)")
                    fk, fq, fr, fa = flat(kq[:, 0, :, :]), flat(kq[:, 1, :, :]), flat(kr[:, :, :]), flat(al[:, :, :])
                    dve.tensor_tensor(fk, fk, fa, ALU.mult)
                    dve.tensor_tensor(fq, fq, fa, ALU.mult).then_inc(s["scaled"], 1)

                    def rescale(l, c):
                        dve.wait_ge(s["scaled"], l + 1)
                        dve.wait_ge(s["products"], l + 1)
                        halves = lambda t: t.rearrange("p (m two c) -> p m two c", two=2, c=c)
                        m = HDP * T // (2 * c)
                        first = halves(fa)[:, :, 0, 0:1].to_broadcast([128, m, c])
                        second = halves(fa)[:, :, 1, 0:1].to_broadcast([128, m, c])
                        for t, half, factor in ((fk, 1, first), (fq, 1, first), (fr, 0, second)):
                            v = halves(t)[:, :, half, :]
                            last = dve.tensor_tensor(v, v, factor, ALU.mult)
                        link(last)
                        dve.tensor_tensor(halves(fa)[:, :, 0, 0:1], halves(fa)[:, :, 0, 0:1], halves(fa)[:, :, 1, 0:1],
                                          ALU.mult).then_inc(s["scaled"], 1)

                    for l, c in enumerate(LEVELS):
                        dve.wait_ge(s["products"], l + 1)
                        if l == 0:
                            dve.wait_ge(s["diag"], 1)
                        if l >= 2:
                            dve.wait_ge(s["w_ps"], l - 1)
                        for bk in range(4):
                            ps = bank[bk][:, :].rearrange("p (u n) -> p u n", n=64)
                            dve.tensor_tensor(wide(aT, bk), ps[:, :, 0:32], level(l), ALU.mult)
                            last = dve.copy_predicated(wide(pc, bk), lmi[:, l, :].unsqueeze(1).to_broadcast([128, PB, 32]),
                                                       ps[:, :, 32:64])
                        last.then_inc(s["masked"], 1)
                        rescale(l, c)
                        dve.wait_ge(s["masked"], l + 1)
                        if l == 0:
                            link(dve.tensor_tensor(XT[:, :, :], lm[:, 5, :].unsqueeze(1).to_broadcast([128, U_, 32]),
                                                   aT[:, :, :], ALU.subtract))
                            dve.transpose(X[:, :, :].rearrange("p u n -> p (u n)"), XT[:, :, :].rearrange("p u n -> p (u n)"))\
                                .then_inc(s["inverse"], 1)
                        else:
                            dve.wait_ge(s["xw_ps"], l)
                            for i in range(2):
                                Xi = X[:, 16 * i:16 * i + 16, :]
                                last = dve.tensor_tensor(Xi, Xi, bank[6 + i][:, :].rearrange("p (u n) -> p u n", n=32),
                                                         ALU.subtract)
                            link(last)
                            dve.transpose(XT[:, :, :].rearrange("p u n -> p (u n)"), X[:, :, :].rearrange("p u n -> p (u n)"))\
                                .then_inc(s["inverse"], 1)
                    dve.wait_ge(s["p_t"], 1)
                    dve.wait_ge(s["w_ps"], len(LEVELS) - 1)
                    for bk in range(4):
                        for par in range(2):
                            r = slice(64 * par, 64 * par + 32)
                            last = dve.tensor_copy(aT[r, bk * PB:(bk + 1) * PB, :],
                                                   bank[bk][r, :].rearrange("p (u n) -> p u n", n=64)[:, :, 0:32])
                    last.then_inc(s["joined"], 1)
                    dve.wait_ge(s["y_ps"], 1)
                    for bk in range(4):
                        last = dve.tensor_copy(wide(U, bk), bank[bk][:, :].rearrange("p (u n) -> p u n", n=64))
                    last.then_inc(s["y"], 1)
                    dve.wait_ge(s["y"], 1)
                    dve.wait_ge(s["u2_ps"], 1)
                    for bk in range(4):
                        for par in range(2):
                            r2 = slice(64 * par + 32, 64 * par + 64)
                            u_ = U[r2, bk * PB:(bk + 1) * PB, :]
                            last = dve.tensor_tensor(u_, u_, bank[bk][r2, :].rearrange("p (u n) -> p u n", n=64),
                                                     ALU.subtract)
                    last.then_inc(s["u"], 1)
                    for n in range(HDP):
                        dve.wait_ge(s["o_norm"], n + 1)
                        link(dve.reciprocal(nb[:, n % 2, :], nb[:, n % 2, :]))
                        dve.scalar_tensor_tensor(oT[:, n, :], bank[4 + n][:, :], col("headw", n), nb[:, n % 2, :], ALU.mult,
                                                 ALU.mult).then_inc(s["o"], 1)
                    dve.wait_ge(s["wo_ps"], 1)
                    dve.wait_ge(s["g2"], 1)
                    link(dve.tensor_tensor(h[:, :], tmp[:, 0, :], bank[2][:, :], ALU.mult))
                    dve.tensor_tensor(h[:, :], h[:, :], z[:, :], ALU.add).then_inc(s["y2"], 1)
                    dve.wait_ge(s["ln_log"], 3)
                    link(dve.reciprocal(rs[:, :], rs[:, :]))
                    dve.wait_ge(s["y2"], 1)
                    dve.scalar_tensor_tensor(z[:, :], h[:, :], col("ffw"), rs[:, :], ALU.mult, ALU.mult).then_inc(s["zz"], 1)
                    for n in range(4):
                        dve.wait_ge(s["ff_silu"], n + 1)
                        dve.tensor_tensor(drive[:, n, :], tmp[:, n % 2, :], bank[4 + n % 2][:, :], ALU.mult)\
                            .then_inc(s["ff"], 1)
                    link(dve.tensor_tensor(xg[:, :], xg[:, :], h[:, :], ALU.add))
                    dve.wait_ge(s["down"], 1)
                    dve.tensor_tensor(xg[:, :], xg[:, :], bank[6][:, :], ALU.add)

            run_stage("delta", LN + "h au_ps au proj proj_read squared norm_ps norm normed pad conv spikes count alpha_pre alpha "
                           "beta_ps beta kr diag_ps diag scaled products masked inverse w_ps w xw_ps join_ps joined "
                           "zeros p_t v_ps v y_ps y r_ps r u2_ps u o_ps o_squared o_norm_ps o_norm o g1_ps g1 g2_ps g2 "
                           "wo_ps y2 zz ff_ps ff_silu ff down dve", body)

        def mlstm(g):
            NB = NHX * NP
            isq = 1.0 / float(np.sqrt(np.float32(DHX)))

            def body(ctx, s, block):
                keep_rows = sb("keep_rows", [NHX, T], ctx=ctx)
                drop_rows = sb("drop_rows", [NHX, T], ctx=ctx)
                f = sb("f_gate", [NHX, T], ctx=ctx)
                lf = sb("log_f", [NHX, T], ctx=ctx)
                cs = sb("cumulated", [NHX, T], ctx=ctx)
                a = sb("gate_a", [NHX, T], ctx=ctx)
                M = sb("running_max", [NHX, T], ctx=ctx)
                m2 = sb("neg_max_log", [NHX, T], ctx=ctx)
                aT = sb("gate_a_t", [128, NP, NHX], ctx=ctx)
                em = sb("exp_neg_max", [128, NP, NHX], ctx=ctx)
                dm = sb("decay", [128, NHX, NP, S], ctx=ctx)
                cT = sb("weights_t", [128, NHX, NP, S], ctx=ctx)
                nrm = sb("normalizer", [128, NP, NHX], ctx=ctx)
                hn = sb("head_out", [128, NP, NHX, DHX], ctx=ctx)
                hq = sb("head_sq", [128, NP, NHX, DHX], ctx=ctx)
                st = sb("head_stat", [128, NP, NHX], ctx=ctx)

                @block.tensor
                def _(pe):
                    ln_pe(pe, s, xg[:, :])
                    pe.wait_ge(s["ln_out"], 1)
                    for gate in range(2):
                        for part in range(3):
                            last = pe.matmul(bank[2 + gate][0:NHX, :],
                                             col("gates", part * 2 * NHX + gate * NHX, NHX), (z if part == 0 else cg)[:, :],
                                             start=part == 0, stop=part == 2)
                    last.then_inc(s["gates"], 1)
                    for h in range(NHX):
                        for b in range(GB):
                            bp, par = divmod(b, 2)
                            last = pe.matmul(bank[4 + h][64 * par:64 * par + 64, bp * S:(bp + 1) * S],
                                             cg[32 * h:32 * h + 32, b * S:(b + 1) * S], z[32 * h:32 * h + 32, b * S:(b + 1) * S],
                                             start=bp == 0, stop=True, skip_group_check=True)
                    last.then_inc(s["qk"], 1)
                    pe.wait_ge(s["rows"], 1)
                    for i, row in enumerate((a, m2)):
                        for bp in range(NP):
                            at = bp * NHX
                            last = pe.transpose(bank[i][:, at:at + NHX], row[:, bp * 128:(bp + 1) * 128],
                                                cst[0:NHX, 2, 0:NHX])
                    last.then_inc(s["columns"], 1)
                    for half in range(2):
                        pe.matmul(bank[2 + half][:, :], identb[:, :], cmT[:, :], start=True, stop=False,
                                  skip_group_check=True)
                        for i in range(2):
                            h = 2 * half + i
                            for par in range(2):
                                rhs = M[:, :].rearrange("p (b c s) -> p b c s", c=2, s=S)[:, :, par, :]
                                last = pe.matmul(bank[2 + half][64 * par:64 * par + 64, i * 256:(i + 1) * 256],
                                                 self_[0:NHX, h, 0:64], rhs, start=False, stop=True,
                                                 skip_group_check=True)
                    last.then_inc(s["neg_max"], 1)
                    pe.wait_ge(s["weights"], NHX)
                    for b in range(GB):
                        bp, par = divmod(b, 2)
                        for h in range(NHX):
                            at = ((bp % 2) * NHX + h) * (DHX + 1)
                            last = pe.matmul(bank[2 + bp // 2][64 * par:64 * par + 64, at:at + DHX + 1],
                                             cT[64 * par:64 * par + 64, h, bp, :], ctk[64 * par:64 * par + 64, bp, h, :],
                                             start=bp % 2 == 0 and h == 0, stop=True, skip_group_check=True)
                    last.then_inc(s["attended"], 1)
                    pe.wait_ge(s["head_out"], 1)
                    for bp in range(NP):
                        last = pe.transpose(bank[1][:, bp * 128:(bp + 1) * 128],
                                            hn[:, bp, :, :].rearrange("p h d -> p (h d)"), IDENT)
                    last.then_inc(s["out_t"], 1)

                @block.gpsimd
                def _(pool):
                    pool.memset(keep_rows[:, :], 1.0)
                    pool.memset(drop_rows[:, :], 0.0).then_inc(s["rows_set"], 1)
                    pool.wait_ge(s["rows_set"], 1)
                    pool.memset(keep_rows[:, 0:T:S], 0.0)
                    pool.memset(drop_rows[:, 0:T:S], NEG).then_inc(s["rows_set"], 1)

                @block.scalar
                def _(act):
                    link = link_of(act, s["act"])
                    ln_act(act, s)
                    act.wait_ge(s["f"], 1)
                    link(act.activation(lf[:, :], f[:, :], ACT.Abs))
                    link(act.activation(lf[:, :], lf[:, :], ACT.Exp, scale=-1.0))
                    act.activation(lf[:, :], lf[:, :], ACT.Ln, bias=1.0).then_inc(s["log"], 1)
                    act.wait_ge(s["columns"], 1)
                    act.activation(em[:, :, :], bank[1][:, 0:NB].rearrange("p (b h) -> p b h", h=NHX), ACT.Exp)\
                        .then_inc(s["exp_max"], 1)
                    for half in range(2):
                        act.wait_ge(s["log_decay"], half + 1)
                        act.activation(dm[:, 2 * half:2 * half + 2, :, :], dm[:, 2 * half:2 * half + 2, :, :], ACT.Exp)\
                            .then_inc(s["decay"], 1)
                    act.wait_ge(s["head_var"], 1)
                    act.activation(st[:, :, :], st[:, :, :], ACT.Sqrt, bias=eps_ap(LN_EPS), scale=1.0 / DHX)\
                        .then_inc(s["head_std"], 1)

                @block.vector
                def _(dve):
                    link = link_of(dve, s["dve"])

                    def bc(t, n=DHX):
                        return t.unsqueeze(3).to_broadcast([128, NP, NHX, n])

                    ln_dve(dve, s, xg[:, :], z[:, :])
                    dve.wait_ge(s["gates"], 1)
                    dve.tensor_scalar(f[:, :], bank[3][0:NHX, :], col("gfb", p=NHX), None, ALU.add).then_inc(s["f"], 1)
                    dve.wait_ge(s["log"], 1)
                    link(dve.scalar_tensor_tensor(lf[:, :], f[:, :], 0.0, lf[:, :], ALU.min, ALU.subtract))
                    dve.wait_ge(s["rows_set"], 2)
                    link(dve.tensor_tensor_scan(cs[:, :], keep_rows[:, :], lf[:, :], 0.0, ALU.mult, ALU.add))
                    link(dve.scalar_tensor_tensor(a[:, :], bank[2][0:NHX, :], col("gib", p=NHX), cs[:, :], ALU.add,
                                                  ALU.subtract))
                    link(dve.tensor_tensor_scan(M[:, :], drop_rows[:, :], a[:, :], 0.0, ALU.add, ALU.max))
                    link(dve.scalar_tensor_tensor(m2[:, :], cs[:, :], -1.0, M[:, :], ALU.mult, ALU.subtract))
                    dve.tensor_scalar(M[:, :], M[:, :], -1.0, None, ALU.mult).then_inc(s["rows"], 1)
                    dve.wait_ge(s["columns"], 1)
                    link(dve.tensor_copy(aT[:, :, :], bank[0][:, 0:NB].rearrange("p (b h) -> p b h", h=NHX)))
                    dve.wait_ge(s["neg_max"], 1)
                    for half in range(2):
                        for i in range(2):
                            h = 2 * half + i
                            last = dve.tensor_tensor(
                                dm[:, h, :, :], bank[2 + half][:, i * 256:(i + 1) * 256].rearrange("p (b s) -> p b s", s=S),
                                aT[:, :, h:h + 1].to_broadcast([128, NP, S]), ALU.add)
                        last.then_inc(s["log_decay"], 1)
                    dve.wait_ge(s["qk"], 1)
                    for h in range(NHX):
                        dve.wait_ge(s["decay"], h // 2 + 1)
                        dve.scalar_tensor_tensor(cT[:, h, :, :], bank[4 + h][:, 0:256].rearrange("p (b s) -> p b s", s=S),
                                                 isq, dm[:, h, :, :], ALU.mult, ALU.mult).then_inc(s["weights"], 1)
                    dve.wait_ge(s["attended"], 1)

                    def attended(i, c0, c1):
                        return bank[2 + i][:, 0:2 * NHX * (DHX + 1)].rearrange("p (b h d) -> p b h d", b=2, d=DHX + 1)[:, :, :, c0:c1]
                    for i in range(2):
                        last = dve.tensor_copy(nrm[:, 2 * i:2 * i + 2, :].unsqueeze(3), attended(i, DHX, DHX + 1))
                    link(last)
                    link(dve.scalar_tensor_tensor(nrm[:, :, :], nrm[:, :, :], -1.0, nrm[:, :, :], ALU.mult, ALU.max))
                    dve.wait_ge(s["exp_max"], 1)
                    link(dve.tensor_tensor(nrm[:, :, :], nrm[:, :, :], em[:, :, :], ALU.max))
                    link(dve.tensor_scalar(nrm[:, :, :], nrm[:, :, :], 1e-6, None, ALU.add))
                    link(dve.reciprocal(nrm[:, :, :], nrm[:, :, :]))
                    for i in range(2):
                        last = dve.tensor_tensor(hn[:, 2 * i:2 * i + 2, :, :], attended(i, 0, DHX),
                                                 nrm[:, 2 * i:2 * i + 2, :].unsqueeze(3).to_broadcast([128, 2, NHX, DHX]),
                                                 ALU.mult)
                    link(last)
                    link(dve.tensor_reduce(st[:, :, :], hn[:, :, :, :], AX, ALU.add))
                    link(dve.tensor_scalar(st[:, :, :], st[:, :, :], 1.0 / DHX, None, ALU.mult))
                    link(dve.tensor_tensor(hn[:, :, :, :], hn[:, :, :, :], bc(st[:, :, :]), ALU.subtract))
                    link(dve.tensor_tensor(hq[:, :, :, :], hn[:, :, :, :], hn[:, :, :, :], ALU.mult))
                    dve.tensor_reduce(st[:, :, :], hq[:, :, :, :], AX, ALU.add).then_inc(s["head_var"], 1)
                    dve.wait_ge(s["head_std"], 1)
                    link(dve.reciprocal(st[:, :, :], st[:, :, :]))
                    link(dve.tensor_tensor(hn[:, :, :, :], hn[:, :, :, :], bc(st[:, :, :]), ALU.mult))
                    dve.tensor_tensor(hn[:, :, :, :].rearrange("p b h d -> p b (h d)"),
                                      hn[:, :, :, :].rearrange("p b h d -> p b (h d)"),
                                      col("outnorm", 0, D).unsqueeze(1).to_broadcast([128, NP, D]), ALU.mult)\
                        .then_inc(s["head_out"], 1)
                    dve.wait_ge(s["out_t"], 1)
                    dve.tensor_tensor(xg[:, :], xg[:, :], bank[1][:, :], ALU.add)

            run_stage("gated", LN + "rows_set gates qk rows columns neg_max weights attended head_out out_t f log exp_max decay "
                           "log_decay head_var head_std act dve", body)

        with nc.Fori(0, NG) as g:
            if "A" in stages:
                attention(g, False)
            else:
                def load(ctx, s, block):
                    @block.sync
                    def _(sp):
                        sp.dma_start(xg[:, :], x[g, :, :]).then_inc(s["x_in"], 16)
                        sp.dma_start(cg[:, :], ctxT[g, :, :]).then_inc(s["x_in"], 16)
                        sp.dma_start(ctk[:, :, :, :], ctx_tok[g, :, :, :, :]).then_inc(s["x_in"], 16)
                        sp.wait_ge(s["x_in"], 48)
                run_stage("load", "x_in", load)
            if "B" in stages:
                attention(g, True)
            if "C" in stages:
                moe0(g)
            if "D" in stages:
                delta(g)
            if "E" in stages:
                mlstm(g)
            if "F" in stages:
                moe1(g)

            def store(ctx, s, block):
                @block.sync
                def _(sp):
                    sp.dma_start(out[g, :, :], xg[:, :]).then_inc(s["stored"], 16)
                    sp.wait_ge(s["stored"], 16)
            run_stage("store", "stored", store)


def _layouts(i):
    f = {k: np.asarray(v) for k, v in i.items()}
    one = lambda v: v.reshape(-1, 1)

    def rows(v):
        return v.reshape(-1, 128).T

    def heads(v):
        out = np.zeros(v.shape[:-1] + (H, 32), np.float32)
        out[..., :8] = v.reshape(v.shape[:-1] + (H, 8))
        return out.reshape(v.shape[:-1] + (H * 32,))

    def down(v, p=128):
        out = np.zeros((128,) + v.shape[1:], np.float32)
        out[:v.shape[0]] = v
        return out

    def all_rows(v):
        return np.tile(v.reshape(1, -1), (128, 1))

    hk = f["L1_attn_beta_spike"].reshape(HD, 64)
    small = {
        "bq": rows(heads(f["L0_xattn_wq_b"])), "bk": rows(heads(f["L0_xattn_wk_b"])),
        "bv": rows(heads(f["L0_xattn_wv_b"])), "bo": one(f["L0_xattn_wo_b"]),
        "norm_in": one(f["L1_attn_norm_in_w"]), "conv_w": f["L1_attn_conv_w"].reshape(128, 4),
        "conv_b": one(f["L1_attn_conv_b"]), "bau": down(one(f["L1_attn_bau"])), "bad": rows(f["L1_attn_bad"]),
        "asp": rows(f["L1_attn_alpha_spike"].reshape(-1)), "bbeta": rows(np.repeat(f["L1_attn_bbeta"], 64)),
        "headw": rows(f["L1_attn_head_norm_w"].reshape(-1)), "bu1": down(one(f["L1_attn_bu1"])),
        "bu2": one(f["L1_attn_bu2"]), "ffw": one(f["L1_attn_ff_norm_w"]),
        "outnorm": all_rows(f["L1_xattn_outnorm_scale"]), "lng": one(f["L1_ffn_ln_g"]), "lnb": one(f["L1_ffn_ln_b"]),
        "rb": all_rows(f["L1_ffn_rb"]), "b1": rows(f["L1_ffn_b1"].reshape(-1)),
        "rank8": all_rows(np.arange(8, 0, -1, dtype=np.float32)),
        "gib": down(one(f["L1_xattn_igate_bias"])), "gfb": down(one(f["L1_xattn_fgate_bias"])),
        "rw0": f["L0_ffn_router_w"].T, "rw1": f["L1_ffn_rW"], "wau": f["L1_attn_Wau"], "wu1": f["L1_attn_Wu1"],
        "wu2": down(f["L1_attn_Wu2"]),
        "gates": np.concatenate([f["L1_xattn_igate_kernel"].reshape(3, 128, 4),
                                 f["L1_xattn_fgate_kernel"].reshape(3, 128, 4)], axis=2)
        .transpose(1, 0, 2).reshape(128, 24),
    }
    small = np.concatenate([small[n].reshape(128, w) for n, w in SMALL], axis=1)

    blocks = np.zeros((128, 128), np.float32)
    blocks[:64, :64] = blocks[64:, 64:] = 1.0
    const = np.stack([np.full((128, 128), 1.0 / 128, np.float32), blocks, np.eye(128, dtype=np.float32)], axis=1)
    t = np.arange(64)
    causal = np.where(t[None, :] > t[:, None], np.float32(NEG), np.float32(0.0))
    causal_t = np.tile(causal.T, (2, 8))
    causal = np.tile(causal, (2, 8))
    j, q = np.arange(32)[:, None], np.arange(32)[None, :]
    level = [((j // (2 * c) == q // (2 * c)) & (j % (2 * c) < c) & (q % (2 * c) >= c)) for c in LEVELS] + [j == q]
    lmask = np.tile(np.stack(level, axis=1).astype(np.float32), (4, 1, 1))
    sel = np.zeros((8, 8, 128), np.float32)
    sel[np.arange(8), np.arange(8)] = 1.0

    w_self = np.stack([f["L0_attn_Wq"], f["L0_attn_Wk"], f["L0_attn_Wv"],
                       f["L0_attn_Wo"].reshape(8, 128, 128).transpose(1, 0, 2).reshape(128, 1024)], axis=1)
    wo = heads(f["L0_xattn_wo_w"]).T.reshape(4, 128, 128).transpose(1, 0, 2).reshape(128, 512)
    w_cross = np.stack([heads(f["L0_xattn_wq_w"].T), heads(f["L0_xattn_wk_w"].T), heads(f["L0_xattn_wv_w"].T), wo], axis=1)
    dn = np.zeros((E0, 384, 128), np.float32)
    dn[:, :I0] = f["L0_ffn_down_w"].transpose(0, 2, 1)
    w_moe0 = np.concatenate([f["L0_ffn_gate_w"].transpose(2, 0, 1), f["L0_ffn_up_w"].transpose(2, 0, 1),
                             dn.reshape(E0, 3, 128, 128).transpose(2, 0, 1, 3).reshape(128, E0, 384)], axis=2)
    beta_rep = np.repeat(f["L1_attn_Wbeta"], 64, axis=1)
    bsp = np.zeros((HDP, 2, 64, 2, 64), np.float32)
    for a in range(2):
        bsp[:, a, :, a, :] = hk.reshape(HDP, 2, 64)[:, a, :, None]
    bsp = bsp.reshape(HDP, 128, 128).transpose(1, 0, 2).reshape(128, 512)
    in_rows = lambda v: v.reshape(4, 128, 128).transpose(1, 0, 2).reshape(128, 512)
    wv = f["L1_attn_Wv"].reshape(128, HDP, 2, 64).transpose(0, 2, 1, 3).reshape(128, 512)
    w_delta = np.stack([f["L1_attn_Wq"], f["L1_attn_Wk"], wv, f["L1_attn_Wspike"], down(f["L1_attn_Wad"]), beta_rep,
                        bsp, in_rows(f["L1_attn_Wo"]), f["L1_attn_Wff1"], f["L1_attn_Wff3"], in_rows(f["L1_attn_Wff2"])],
                       axis=1)
    w_moe1 = np.concatenate([f["L1_ffn_W1"].transpose(1, 0, 2),
                             f["L1_ffn_W2"].reshape(E1, 2, 128, 128).transpose(2, 0, 1, 3).reshape(128, E1, 256)], axis=2)

    def grouped(v):
        return v.reshape(NG, T, D).transpose(0, 2, 1)

    ctx_tok = np.ones((NG, 128, NP, NHX, DHX + 1), np.float32)
    ctx_tok[..., :DHX] = f["ctx_1024"].reshape(NG, NP, 128, NHX, DHX).transpose(0, 2, 1, 3, 4)
    return {"x": grouped(f["x"]), "ctxT": grouped(f["ctx_1024"]), "ctx_tok": ctx_tok, "small": small, "const": const,
            "cmask": causal, "cmaskT": causal_t, "lmask": lmask, "sel": sel, "w_self": w_self, "w_cross": w_cross, "w_moe0": w_moe0,
            "w_delta": w_delta, "w_moe1": w_moe1, "b2": f["L1_ffn_b2"]}


def kernel(**inputs):
    import concourse.bacc as _bacc
    from concourse.bass_utils import run_bass_kernel_spmd as _run

    nc = _bacc.Bacc("TRN2", target_bir_lowering=False, num_devices=1)
    arrays, args = {}, []
    for name, a in _layouts(inputs).items():
        a = np.ascontiguousarray(a)
        arrays[f"in_{name}_dram"] = a
        args.append(nc.dram_tensor(f"in_{name}_dram", a.shape, F32, kind="ExternalInput").ap())
    args.append(nc.dram_tensor("out_dram", (NG, D, T), F32, kind="ExternalOutput").ap())
    build(nc, *args)
    r = _run(nc, [arrays], core_ids=[0])
    return r.results[0]["out_dram"].transpose(0, 2, 1).reshape(B, S, D)
```

```python
from contextlib import ExitStack

import numpy as np
import concourse.bass as bass
from concourse import mybir

F32 = mybir.dt.float32
BF16 = mybir.dt.bfloat16
U8 = mybir.dt.uint8
ALU = mybir.AluOpType
ACT = mybir.ActivationFunctionType
AX = mybir.AxisListType.X

B, S, D = 64, 64, 128
GB = 8
NG = B // GB
T = GB * S
NP = GB // 2
H = 16
HP = H // 2
E0, I0 = 8, 352
I0_TILES = [(0, 128), (128, 128), (256, 96)]
HD = 8
HDP = HD // 2
E1, F1 = 8, 256
NHX, DHX = 4, 32
LEVELS = [1, 2, 4, 8, 16]
NEG = -1.0e30
LN_EPS, RMS_EPS = 1e-5, 1e-6

SMALL = [("bq", 4), ("bk", 4), ("bv", 4), ("bo", 1), ("norm_in", 1), ("conv_w", 4), ("conv_b", 1), ("bau", 1),
         ("bad", HDP), ("asp", HDP), ("bbeta", HDP), ("headw", HDP), ("bu1", 1), ("bu2", 1), ("ffw", 1),
         ("outnorm", D), ("lng", 1), ("lnb", 1), ("rb", E1), ("b1", 2 * E1), ("rank8", 8),
         ("gib", 1), ("gfb", 1), ("rw0", E0), ("rw1", E1), ("wau", 64), ("wu1", 64), ("wu2", 128), ("gates", 6 * NHX), ("norm_rows", 128)]
SMALL_AT, _at = {}, 0
for _n, _w in SMALL:
    SMALL_AT[_n] = (_at, _w)
    _at += _w
N_SMALL = _at
CONST = ["mean", "blocksum", "ident"]


def link_of(eng, sem):
    count = [0]

    def link(ins):
        count[0] += 1
        ins.then_inc(sem, 1)
        eng.wait_ge(sem, count[0])
    return link


def build(nc, x, ctxT, ctx_tok, small, const, cmask, cmaskT, lmask, sel, norm_sel, w_self, w_cross, w_moe0, w_delta, w_moe1, b2, out,
          stages="ABCDEF"):
    with ExitStack() as top:
        stage = [""]

        def sb(name, shape, dt=F32, ctx=top):
            return ctx.enter_context(nc.sbuf_tensor(f"{stage[0]}{name}", shape, dt))

        bank = [top.enter_context(nc.psum_tensor(f"bank{i}", [128, 512], F32)) for i in range(8)]
        sm = sb("small_sb", [128, N_SMALL])
        cst = sb("const_sb", [128, len(CONST), 128])
        cm = sb("causal_sb", [128, 512], BF16)
        lm = sb("level_sb", [128, 6, 32], F32)
        lmi = sb("level_int_sb", [128, 6, 32], U8)
        cmT = sb("causal_t_sb", [128, 512], BF16)
        identb = sb("ident_bf", [128, 128], BF16)
        selb = sb("sel_bf", [8, 8, 128], BF16)
        self_ = sb("sel_f", [8, 8, 128])
        nsel = sb("norm_sel", [16, 8, 128])
        wA = sb("w_self_sb", [128, 4, 1024])
        wB = sb("w_cross_sb", [128, 4, 512])
        wC = sb("w_moe0_sb", [128, E0, 2 * I0 + 3 * 128])
        wD = sb("w_delta_sb", [128, 11, 512])
        wF = sb("w_moe1_sb", [128, E1, 512])
        b2s = sb("b2_sb", [8, 128])
        xg = sb("x_group", [128, T])
        cg = sb("ctx_group", [128, T])
        ctk = sb("ctx_tokens", [128, NP, NHX, DHX + 1])
        xc = sb("centred", [128, T])
        sq = sb("squared", [128, T])
        rs = sb("rstd", [128, T])
        z = sb("normed", [128, T])

        def col(name, i=0, n=1, p=128):
            at, _ = SMALL_AT[name]
            return sm[0:p, at + i:at + i + n]

        MEAN, BLOCKSUM, IDENT = (cst[:, i, :] for i in range(3))

        with ExitStack() as ctx:
            loaded = ctx.enter_context(nc.semaphore("weights_loaded"))
            with nc.Block() as block:
                @block.sync
                def _(sp):
                    loads = [(sm[:, :], small), (cst[:, :, :], const), (self_[:, :, :], sel), (b2s[:, :], b2),
                             (lm[:, :, :], lmask), (nsel[:, :, :], norm_sel), (wA[:, :, :], w_self), (wB[:, :, :], w_cross),
                             (wC[:, :, :], w_moe0), (wD[:, :, :], w_delta), (wF[:, :, :], w_moe1)]
                    for dst, src in loads:
                        sp.dma_start(dst, src).then_inc(loaded, 16)
                    sp.dma_start(xc[:, :], cmask).then_inc(loaded, 16)
                    sp.dma_start(sq[:, :], cmaskT).then_inc(loaded, 16)
                    sp.wait_ge(loaded, 16 * 13)

                @block.vector
                def _(v):
                    v.wait_ge(loaded, 16 * 13)
                    v.tensor_copy(cm[:, :], xc[:, :])
                    v.tensor_copy(cmT[:, :], sq[:, :])
                    v.tensor_copy(identb[:, :], IDENT)
                    v.tensor_copy(selb[:, :, :], self_[:, :, :])
                    v.tensor_copy(lmi[:, :, :], lm[:, :, :])
            nc.all_engine_barrier(sems_to_clear=loaded)

        def run_stage(tag, names, body):
            stage[0] = tag + "_"
            with ExitStack() as ctx:
                s = {n: ctx.enter_context(nc.semaphore(f"{tag}_{n}")) for n in names.split()}
                with nc.Block() as block:
                    body(ctx, s, block)
                numbers = [x.num for x in s.values()]
                nc.all_engine_barrier(sems_to_clear=range(min(numbers), max(numbers) + 1))

        LN = "ln_mean ln_centred ln_squared ln_var ln_std ln_rstd ln_out "
        HALVES = [slice(0, T // 2), slice(T // 2, T)]
        MEAN_BANKS, VAR_BANKS = (0, 2), (1, 3)

        def nth(n, k):
            return 2 * (n - 1) + k + 1

        def ln_pe(pe, s, src, n=1, rms=False):
            if not rms:
                for k, c in enumerate(HALVES):
                    pe.matmul(bank[MEAN_BANKS[k]][:, c], MEAN, src[:, c], start=True, stop=True).then_inc(s["ln_mean"], 1)
            for k, c in enumerate(HALVES):
                pe.wait_ge(s["ln_squared"], nth(n, k))
                pe.matmul(bank[VAR_BANKS[k]][:, c], MEAN, sq[:, c], start=True, stop=True).then_inc(s["ln_var"], 1)

        def ln_act(act, s, src=None, n=1, rms=False, eps=LN_EPS, then=None):
            act.preload_act_table(ACT.Sqrt)
            for k, c in enumerate(HALVES):
                if not rms:
                    act.wait_ge(s["ln_centred"], nth(n, k))
                act.activation(sq[:, c], src[:, c] if rms else xc[:, c], ACT.Square).then_inc(s["ln_squared"], 1)
            for k, c in enumerate(HALVES):
                act.wait_ge(s["ln_var"], nth(n, k))
                act.activation(rs[:, c], bank[VAR_BANKS[k]][:, c], ACT.Sqrt, bias=eps_tiles[eps]).then_inc(s["ln_std"], 1)
            if then is not None:
                act.preload_act_table(then)

        eps_tiles = {}

        def ln_reciprocal(dve, s, n):
            for k, c in enumerate(HALVES):
                dve.wait_ge(s["ln_std"], nth(n, k))
                dve.reciprocal(rs[:, c], rs[:, c]).then_inc(s["ln_rstd"], 1)

        def ln_dve(dve, s, src, dst, n=1):
            for k, c in enumerate(HALVES):
                dve.wait_ge(s["ln_mean"], nth(n, k))
                dve.tensor_tensor(xc[:, c], src[:, c], bank[MEAN_BANKS[k]][:, c], ALU.subtract).then_inc(s["ln_centred"], 1)
            ln_reciprocal(dve, s, n)
            for k, c in enumerate(HALVES):
                dve.wait_ge(s["ln_rstd"], nth(n, k))
                last = dve.tensor_tensor(dst[:, c], xc[:, c], rs[:, c], ALU.mult)
            last.then_inc(s["ln_out"], 1)

        for eps in (LN_EPS, RMS_EPS):
            eps_tiles[eps] = sb(f"eps{len(eps_tiles)}", [128, 1])[:, :]
        with nc.Block() as block:
            @block.vector
            def _(v):
                for eps, tile in eps_tiles.items():
                    v.memset(tile, eps)

        def attention(g, cross):
            NT = 4 if cross else 8
            W = 512 if cross else 1024
            VW = 32 if cross else 64
            w = wB if cross else wA
            n_proj = 2 * NT + NP * (W // 512)
            NU = NP * 2
            scale = 1.0 / np.sqrt(8.0) if cross else 1.0 / np.sqrt(64.0)

            def heads_of(half, i):
                pair = half + 2 * i if cross else 4 * half + i
                return pair

            def body(ctx, s, block):
                qT = sb("queries", [128, NT, T], ctx=ctx)
                kT = sb("keys", [128, NT, T], ctx=ctx)
                val = sb("values", [128, NP, W], ctx=ctx)
                oT = sb("attended", [128, NT, T], ctx=ctx)
                p = sb("probs", [128, 2, 512], ctx=ctx)
                pT = sb("probs_t", [128, 2, 512], ctx=ctx)
                mx = sb("row_max", [128, 2, 8], ctx=ctx)
                sums = sb("row_sum", [128, 2, 8], ctx=ctx)

                def projection(j):
                    src = cg if cross else z
                    if j < NT:
                        return w[:, 0, j * 128:(j + 1) * 128], z[:, :], qT[:, j, :], ("bq", j)
                    if j < 2 * NT:
                        m = j - NT
                        return w[:, 1, m * 128:(m + 1) * 128], src[:, :], kT[:, m, :], ("bk", m)
                    m, c = divmod(j - 2 * NT, W // 512)
                    return src[:, m * 128:(m + 1) * 128], w[:, 2, c * 512:(c + 1) * 512], \
                        val[:, m, c * 512:(c + 1) * 512], None

                if not cross:
                    @block.sync
                    def _(sp):
                        sp.dma_start(xg[:, :], x[g, :, :]).then_inc(s["x_in"], 16)
                        sp.dma_start(cg[:, :], ctxT[g, :, :]).then_inc(s["x_in"], 16)
                        sp.dma_start(ctk[:, :, :, :], ctx_tok[g, :, :, :, :]).then_inc(s["x_in"], 16)
                        sp.wait_ge(s["x_in"], 48)

                @block.tensor
                def _(pe):
                    if not cross:
                        pe.wait_ge(s["x_in"], 48)
                    ln_pe(pe, s, xg[:, :])
                    pe.wait_ge(s["ln_out"], 1)
                    for j in range(n_proj):
                        if j >= 2:
                            pe.wait_ge(s["proj_evac_act" if j % 2 == 0 else "proj_evac_dve"], j // 2)
                        lhsT, rhs, _, _ = projection(j)
                        pe.matmul(bank[j % 2][:, :], lhsT, rhs, start=True, stop=True).then_inc(s["proj"], 1)
                    pe.wait_ge(s["proj_evac_act"], (n_proj + 1) // 2)
                    pe.wait_ge(s["proj_evac_dve"], n_proj // 2)

                    def scores(u):
                        bp, half = divmod(u, 2)
                        if u >= 2:
                            pe.wait_ge(s["shifted"], u - 1)
                        ps = bank[2 + u % 2]
                        if not cross:
                            pe.matmul(ps[:, :], identb[:, :], cm[:, :], start=True, stop=False, skip_group_check=True)
                        for i in range(4):
                            pair = heads_of(half, i)
                            for b in range(2):
                                for par in range(2):
                                    h = 2 * pair + par
                                    r0, tile, k = (32 * (h % 4), h // 4, 32) if cross else (64 * par, pair, 64)
                                    tok = (2 * bp + b) * S
                                    last = pe.matmul(ps[64 * par:64 * par + 64, i * 128 + b * 64:i * 128 + b * 64 + 64],
                                                     qT[r0:r0 + k, tile, tok:tok + S], kT[r0:r0 + k, tile, tok:tok + S],
                                                     start=cross and i == 0 and b == 0, stop=True, skip_group_check=True)
                        last.then_inc(s["scores"], 1)

                    def transposed(u):
                        pe.wait_ge(s["probs"], u + 1)
                        if u >= 2:
                            pe.wait_ge(s["probs_t_evac"], u - 1)
                        for i in range(4):
                            last = pe.transpose(bank[4 + u % 2][:, i * 128:(i + 1) * 128],
                                                p[:, u % 2, i * 128:(i + 1) * 128], IDENT)
                        last.then_inc(s["probs_t"], 1)

                    def values(u):
                        bp, half = divmod(u, 2)
                        pe.wait_ge(s["probs_t_evac"], u + 1)
                        if u >= 1:
                            pe.wait_ge(s["out_evac"], u)
                        for i in range(4):
                            pair = heads_of(half, i)
                            for b in range(2):
                                for par in range(2):
                                    h = 2 * pair + par
                                    r0 = 32 * (h % 4) if cross else 64 * par
                                    last = pe.matmul(bank[6 + b][r0:r0 + VW, i * 64:i * 64 + 64],
                                                     val[64 * b:64 * b + 64, bp, h * VW:(h + 1) * VW],
                                                     pT[64 * b:64 * b + 64, u % 2, i * 128 + par * 64:i * 128 + par * 64 + 64],
                                                     start=i == 0, stop=True, skip_group_check=True)
                        last.then_inc(s["attended"], 1)

                    scores(0)
                    scores(1)
                    for u in range(NU):
                        transposed(u)
                        if u + 2 < NU:
                            scores(u + 2)
                        values(u)
                    pe.wait_ge(s["out_evac"], NU + cross)
                    for m in range(NT):
                        wo = w[:, 3, m * 128:(m + 1) * 128]
                        last = pe.matmul(bank[0][:, :], wo, oT[:, m, :], start=m == 0, stop=m == NT - 1)
                    last.then_inc(s["out"], 1)

                @block.scalar
                def _(act):
                    ln_act(act, s, then=ACT.Exp)
                    for j in range(0, n_proj, 2):
                        act.wait_ge(s["proj"], j + 1)
                        _, _, dst, bias = projection(j)
                        if cross and bias:
                            act.activation(dst, bank[0][:, :], ACT.Identity, bias=col(*bias)).then_inc(s["proj_evac_act"], 1)
                        else:
                            act.activation(dst, bank[0][:, :], ACT.Copy).then_inc(s["proj_evac_act"], 1)

                    def pt_evac(u):
                        act.wait_ge(s["probs_t"], u + 1)
                        if u >= 2:
                            act.wait_ge(s["attended"], u - 1)
                        act.activation(pT[:, u % 2, :], bank[4 + u % 2][:, :], ACT.Copy).then_inc(s["probs_t_evac"], 1)

                    for u in range(NU):
                        act.wait_ge(s["shifted"], u + 1)
                        act.activation(p[:, u % 2, :], p[:, u % 2, :], ACT.Exp, scale=float(scale)).then_inc(s["exp"], 1)
                        if u >= 1:
                            pt_evac(u - 1)
                    pt_evac(NU - 1)

                @block.vector
                def _(dve):
                    ln_dve(dve, s, xg[:, :], z[:, :])
                    for j in range(1, n_proj, 2):
                        dve.wait_ge(s["proj"], j + 1)
                        _, _, dst, bias = projection(j)
                        if cross and bias:
                            dve.tensor_scalar(dst, bank[1][:, :], col(*bias), None, ALU.add).then_inc(s["proj_evac_dve"], 1)
                        else:
                            dve.tensor_copy(dst, bank[1][:, :]).then_inc(s["proj_evac_dve"], 1)

                    def evac(u):
                        bp, half = divmod(u, 2)
                        dve.wait_ge(s["attended"], u + 1)
                        for b in range(2):
                            tok = (2 * bp + b) * S
                            if cross:
                                r = slice(64 * half, 64 * half + 64)
                                dst, src = oT[r, 0:4, tok:tok + S], bank[6 + b][r, 0:256]
                            else:
                                dst, src = oT[:, 4 * half:4 * half + 4, tok:tok + S], bank[6 + b][:, 0:256]
                            last = dve.tensor_copy(dst, src.rearrange("p (i t) -> p i t", t=S))
                        last.then_inc(s["out_evac"], 1)

                    def shift(u):
                        i = u % 2
                        ps = bank[2 + i][:, :].rearrange("p (h k) -> p h k", k=S)
                        pr = p[:, i, :].rearrange("p (h k) -> p h k", k=S)
                        dve.wait_ge(s["scores"], u + 1)
                        dve.tensor_reduce(mx[:, i, :], ps, AX, ALU.max).then_inc(s["max"], 1)
                        dve.wait_ge(s["max"], u + 1)
                        if u >= 2:
                            dve.wait_ge(s["probs_t"], u - 1)
                        dve.tensor_tensor(pr, ps, mx[:, i, :].unsqueeze(2).to_broadcast([128, 8, S]), ALU.subtract)\
                            .then_inc(s["shifted"], 1)

                    shift(0)
                    for u in range(NU):
                        if u + 1 < NU:
                            shift(u + 1)
                        i = u % 2
                        pr = p[:, i, :].rearrange("p (h k) -> p h k", k=S)
                        dve.wait_ge(s["exp"], u + 1)
                        dve.tensor_reduce(sums[:, i, :], pr, AX, ALU.add).then_inc(s["sum"], 1)
                        dve.wait_ge(s["sum"], u + 1)
                        dve.reciprocal(sums[:, i, :], sums[:, i, :]).then_inc(s["rsum"], 1)
                        if u >= 1:
                            evac(u - 1)
                    evac(NU - 1)
                    if cross:
                        dve.wait_ge(s["out_evac"], NU)
                        for m in range(NT):
                            last = dve.tensor_scalar(oT[:, m, :], oT[:, m, :], col("bv", m), None, ALU.add)
                        last.then_inc(s["out_evac"], 1)
                    dve.wait_ge(s["out"], 1)
                    if cross:
                        dve.scalar_tensor_tensor(xg[:, :], bank[0][:, :], col("bo"), xg[:, :], ALU.add, ALU.add)
                    else:
                        dve.tensor_tensor(xg[:, :], xg[:, :], bank[0][:, :], ALU.add)

                @block.gpsimd
                def _(pool):
                    for u in range(NU):
                        i = u % 2
                        pr = p[:, i, :].rearrange("p (h k) -> p h k", k=S)
                        pool.wait_ge(s["rsum"], u + 1)
                        pool.tensor_tensor(pr, pr, sums[:, i, :].unsqueeze(2).to_broadcast([128, 8, S]), ALU.mult)\
                            .then_inc(s["probs"], 1)

            run_stage("cross" if cross else "self", LN + "x_in proj proj_evac_act proj_evac_dve scores max shifted exp sum rsum probs probs_t "
                           "probs_t_evac attended out_evac out", body)

        def moe0(g):
            NT = len(I0_TILES)

            def body(ctx, s, block):
                oh = sb("one_hot", [128, 4, E0], ctx=ctx)
                rank = sb("rank", [128, 4, E0], ctx=ctx)
                m1 = sb("best", [128, 4], ctx=ctx)
                ohT = sb("one_hot_t", [E0, T], BF16, ctx=ctx)
                ze = sb("z_expert", [128, 2, T], ctx=ctx)
                sg = sb("silu_gate", [128, 2, T], ctx=ctx)
                h = sb("hidden", [128, 2, T], ctx=ctx)
                steps = [(e, i) for e in range(E0) for i in range(NT)]

                @block.tensor
                def _(pe):
                    ln_pe(pe, s, xg[:, :])
                    pe.wait_ge(s["ln_out"], 1)
                    for i in range(4):
                        last = pe.matmul(bank[2][:, i * E0:(i + 1) * E0], z[:, i * 128:(i + 1) * 128], col("rw0", 0, E0),
                                         start=True, stop=True, skip_group_check=True)
                    last.then_inc(s["logits"], 1)
                    pe.wait_ge(s["one_hot"], 1)
                    for i in range(4):
                        last = pe.transpose(bank[3][0:E0, i * 128:(i + 1) * 128], oh[:, i, :], IDENT)
                    last.then_inc(s["one_hot_ps"], 1)
                    pe.wait_ge(s["one_hot_t"], 1)

                    def down(k):
                        e, i = steps[k]
                        n = I0_TILES[i][1]
                        pe.wait_ge(s["hidden"], k + 1)
                        pe.matmul(bank[7][:, :], wC[0:n, e, 2 * I0 + i * 128:2 * I0 + (i + 1) * 128], h[0:n, k % 2, :],
                                  start=k == 0, stop=k == len(steps) - 1).then_inc(s["down"], 1)

                    def bcast(e):
                        if e >= 1:
                            pe.wait_ge(s["masked"], e)
                        pe.matmul(bank[2][:, :], selb[:, e, :], ohT[:, :], start=True, stop=True).then_inc(s["bcast"], 1)

                    bcast(0)
                    for k, (e, i) in enumerate(steps):
                        if i == 0:
                            pe.wait_ge(s["masked"], e + 1)
                        if i == 1 and e + 1 < E0:
                            bcast(e + 1)
                        if k >= 2:
                            pe.wait_ge(s["hidden"], k - 1)
                        at, n = I0_TILES[i]
                        pe.matmul(bank[3 + k % 2][0:n, :], wC[:, e, at:at + n], ze[:, e % 2, :], start=True, stop=True)\
                            .then_inc(s["gate"], 1)
                        pe.matmul(bank[5 + k % 2][0:n, :], wC[:, e, I0 + at:I0 + at + n], ze[:, e % 2, :], start=True,
                                  stop=True).then_inc(s["up"], 1)
                        if k >= 1:
                            down(k - 1)
                    down(len(steps) - 1)

                @block.scalar
                def _(act):
                    ln_act(act, s, then=ACT.Silu)
                    for k, (e, i) in enumerate(steps):
                        n = I0_TILES[i][1]
                        act.wait_ge(s["gate"], k + 1)
                        if k >= 2:
                            act.wait_ge(s["hidden"], k - 1)
                        act.activation(sg[0:n, k % 2, :], bank[3 + k % 2][0:n, :], ACT.Silu).then_inc(s["silu"], 1)

                @block.vector
                def _(dve):
                    link = link_of(dve, s["dve"])
                    ln_dve(dve, s, xg[:, :], z[:, :])
                    lg = bank[2][:, 0:4 * E0].rearrange("p (i e) -> p i e", e=E0)
                    dve.wait_ge(s["logits"], 1)
                    link(dve.tensor_reduce(m1[:, :], lg, AX, ALU.max))
                    link(dve.tensor_tensor(oh[:, :, :], lg, m1[:, :].unsqueeze(2).to_broadcast([128, 4, E0]), ALU.is_equal))
                    link(dve.tensor_tensor(rank[:, :, :], oh[:, :, :],
                                           col("rank8", 0, 8).unsqueeze(1).to_broadcast([128, 4, E0]), ALU.mult))
                    link(dve.tensor_reduce(m1[:, :], rank[:, :, :], AX, ALU.max))
                    dve.tensor_tensor(oh[:, :, :], rank[:, :, :], m1[:, :].unsqueeze(2).to_broadcast([128, 4, E0]),
                                      ALU.is_equal).then_inc(s["one_hot"], 1)
                    dve.wait_ge(s["one_hot_ps"], 1)
                    dve.tensor_copy(ohT[:, :], bank[3][0:E0, :]).then_inc(s["one_hot_t"], 1)

                    def mask(e):
                        dve.wait_ge(s["bcast"], e + 1)
                        if e >= 2:
                            dve.wait_ge(s["up"], NT * (e - 1))
                        dve.tensor_tensor(ze[:, e % 2, :], z[:, :], bank[2][:, :], ALU.mult).then_inc(s["masked"], 1)

                    mask(0)
                    for k, (e, i) in enumerate(steps):
                        n = I0_TILES[i][1]
                        if i == 2 and e + 1 < E0:
                            mask(e + 1)
                        dve.wait_ge(s["silu"], k + 1)
                        dve.wait_ge(s["up"], k + 1)
                        if k >= 2:
                            dve.wait_ge(s["down"], k - 1)
                        dve.tensor_tensor(h[0:n, k % 2, :], sg[0:n, k % 2, :], bank[5 + k % 2][0:n, :], ALU.mult)\
                            .then_inc(s["hidden"], 1)
                    dve.wait_ge(s["down"], len(steps))
                    dve.tensor_tensor(xg[:, :], xg[:, :], bank[7][:, :], ALU.add)

            run_stage("moe0", LN + "logits one_hot one_hot_ps one_hot_t bcast masked gate up silu hidden down dve", body)

        def moe1(g):
            def body(ctx, s, block):
                z2 = sb("z2", [128, T], ctx=ctx)
                p = sb("gate_probs", [128, 4, E1], ctx=ctx)
                rank = sb("rank", [128, 4, E1], ctx=ctx)
                oh = sb("one_hot", [128, 4, E1], ctx=ctx)
                keep = sb("kept", [128, 4, E1], ctx=ctx)
                m1 = sb("best", [128, 4], ctx=ctx)
                wT = sb("weights_t", [E1, T], ctx=ctx)
                wbc = sb("weight_bc", [128, 2, T], ctx=ctx)
                hid = sb("hid", [128, 2 * E1, T], ctx=ctx)
                h = sb("hidden", [128, 2, T], ctx=ctx)
                steps = [(e, i) for e in range(E1) for i in range(2)]

                def bc(t):
                    return t[:, :].unsqueeze(2).to_broadcast([128, 4, E1])

                @block.tensor
                def _(pe):
                    ln_pe(pe, s, xg[:, :])
                    pe.wait_ge(s["ln_out"], 1)
                    ln_pe(pe, s, z[:, :], n=2)
                    pe.wait_ge(s["z2"], 1)
                    for i in range(4):
                        last = pe.matmul(bank[2][:, i * E1:(i + 1) * E1], z2[:, i * 128:(i + 1) * 128], col("rw1", 0, E1),
                                         start=True, stop=True, skip_group_check=True)
                    last.then_inc(s["logits"], 1)
                    for k, (e, i) in enumerate(steps):
                        if k >= 2:
                            pe.wait_ge(s["gelu"], k - 1)
                        pe.matmul(bank[4 + k % 2][:, :], wF[:, e, i * 128:(i + 1) * 128], z2[:, :], start=True, stop=True)\
                            .then_inc(s["up"], 1)
                    pe.wait_ge(s["weights"], 1)
                    for i in range(4):
                        last = pe.transpose(bank[3][0:E1, i * 128:(i + 1) * 128], p[:, i, :], IDENT)
                    last.then_inc(s["weights_ps"], 1)
                    pe.wait_ge(s["weights_t"], 1)
                    pe.matmul(bank[7][:, :], b2s[:, :], wT[:, :], start=True, stop=False)

                    def down(k):
                        e, i = steps[k]
                        pe.wait_ge(s["hidden"], k + 1)
                        pe.matmul(bank[7][:, :], wF[:, e, 256 + i * 128:256 + (i + 1) * 128], h[:, k % 2, :],
                                  start=False, stop=k == len(steps) - 1).then_inc(s["down"], 1)

                    for k, (e, i) in enumerate(steps):
                        if i == 0:
                            if e >= 2:
                                pe.wait_ge(s["hidden"], 2 * (e - 1))
                            pe.matmul(bank[2 + e % 2][:, :], self_[:, e, :], wT[:, :], start=True, stop=True)\
                                .then_inc(s["bcast"], 1)
                        if k >= 1:
                            down(k - 1)
                    down(len(steps) - 1)

                @block.scalar
                def _(act):
                    ln_act(act, s)
                    ln_act(act, s, n=2, then=ACT.Exp)
                    act.wait_ge(s["shifted"], 1)
                    act.activation(p[:, :, :], p[:, :, :], ACT.Exp).then_inc(s["exp"], 1)
                    act.preload_act_table(ACT.Gelu)
                    for k, (e, i) in enumerate(steps):
                        act.wait_ge(s["up"], k + 1)
                        act.activation(hid[:, k, :], bank[4 + k % 2][:, :], ACT.Gelu, bias=col("b1", 2 * e + i))\
                            .then_inc(s["gelu"], 1)

                @block.vector
                def _(dve):
                    link = link_of(dve, s["dve"])
                    ln_dve(dve, s, xg[:, :], z[:, :])
                    dve.wait_ge(s["ln_out"], 1)
                    ln_dve(dve, s, z[:, :], z2[:, :], n=2)
                    dve.wait_ge(s["ln_out"], 2)
                    dve.tensor_scalar(z2[:, :], z2[:, :], col("lng"), col("lnb"), ALU.mult, ALU.add).then_inc(s["z2"], 1)
                    dve.wait_ge(s["logits"], 1)
                    lg = bank[2][:, 0:4 * E1].rearrange("p (i e) -> p i e", e=E1)
                    link(dve.tensor_tensor(p[:, :, :], lg, col("rb", 0, E1).unsqueeze(1).to_broadcast([128, 4, E1]), ALU.add))
                    link(dve.tensor_reduce(m1[:, :], p[:, :, :], AX, ALU.max))
                    dve.tensor_tensor(p[:, :, :], p[:, :, :], bc(m1), ALU.subtract).then_inc(s["shifted"], 1)
                    dve.wait_ge(s["exp"], 1)
                    link(dve.tensor_reduce(m1[:, :], p[:, :, :], AX, ALU.add))
                    link(dve.reciprocal(m1[:, :], m1[:, :]))
                    link(dve.tensor_tensor(p[:, :, :], p[:, :, :], bc(m1), ALU.mult))
                    link(dve.tensor_copy(keep[:, :, :], p[:, :, :]))
                    for r in range(2):
                        link(dve.tensor_reduce(m1[:, :], keep[:, :, :], AX, ALU.max))
                        link(dve.tensor_tensor(oh[:, :, :], keep[:, :, :], bc(m1), ALU.is_equal))
                        link(dve.tensor_tensor(rank[:, :, :], oh[:, :, :],
                                               col("rank8", 0, 8).unsqueeze(1).to_broadcast([128, 4, E1]), ALU.mult))
                        link(dve.tensor_reduce(m1[:, :], rank[:, :, :], AX, ALU.max))
                        link(dve.tensor_tensor(oh[:, :, :], rank[:, :, :], bc(m1), ALU.is_equal))
                        link(dve.scalar_tensor_tensor(keep[:, :, :], oh[:, :, :], -2.0, keep[:, :, :], ALU.mult, ALU.add))
                    link(dve.scalar_tensor_tensor(p[:, :, :], keep[:, :, :], 0.0, p[:, :, :], ALU.is_lt, ALU.mult))
                    link(dve.tensor_reduce(m1[:, :], p[:, :, :], AX, ALU.add))
                    link(dve.tensor_scalar(m1[:, :], m1[:, :], 1e-8, None, ALU.max))
                    link(dve.reciprocal(m1[:, :], m1[:, :]))
                    dve.tensor_tensor(p[:, :, :], p[:, :, :], bc(m1), ALU.mult).then_inc(s["weights"], 1)
                    dve.wait_ge(s["weights_ps"], 1)
                    dve.tensor_copy(wT[:, :], bank[3][0:E1, :]).then_inc(s["weights_t"], 1)
                    for k, (e, i) in enumerate(steps):
                        dve.wait_ge(s["bcast"], e + 1)
                        dve.wait_ge(s["gelu"], k + 1)
                        if k >= 2:
                            dve.wait_ge(s["down"], k - 1)
                        dve.tensor_tensor(h[:, k % 2, :], hid[:, k, :], bank[2 + e % 2][:, :], ALU.mult)\
                            .then_inc(s["hidden"], 1)
                    dve.wait_ge(s["down"], len(steps))
                    link(dve.tensor_tensor(xg[:, :], xg[:, :], bank[7][:, :], ALU.add))
                    dve.tensor_tensor(xg[:, :], xg[:, :], z[:, :], ALU.add).then_inc(s["x_out"], 1)

            run_stage("moe1", LN + "z2 logits shifted exp weights weights_ps weights_t bcast up gelu hidden down dve x_out", body)

        def delta(g):
            U_ = GB * HDP
            PB = 8

            NORM_ORDER = [4, 5, 6, 7, 0, 1, 2, 3]

            def body(ctx, s, block):
                h = sb("conv_out", [128, T], ctx=ctx)
                au = rs[0:64, :]
                gate, nrm = xc, sq[0:16, :]
                tmp = sb("tmp", [128, 2, T], ctx=ctx)
                nb = sb("beta", [128, 2, T], ctx=ctx)
                mem = sb("membrane", [128, HDP, GB], ctx=ctx)
                spike = sb("spike", [128, HDP, T], ctx=ctx)
                drive = sb("drive", [128, HDP, T], ctx=ctx)
                hc = drive[:, :, :].rearrange("p h t -> p (h t)")[:, 0:GB * (S + 3)].rearrange("p (b t) -> p b t", t=S + 3)
                al = sb("decays", [128, HDP, T], ctx=ctx)
                kq = sb("scaled_kq", [128, 2, HDP, T], ctx=ctx)
                kr = sb("scaled_beta_k", [128, HDP, T], ctx=ctx)
                aT = sb("level_a_t", [128, U_, 32], ctx=ctx)
                X = sb("inverse", [128, U_, 32], ctx=ctx)
                XT = sb("inverse_t", [128, U_, 32], ctx=ctx)
                W = sb("a_times_inverse", [128, U_, 32], ctx=ctx)
                pc = sb("p_t_blocks", [128, U_, 32], ctx=ctx)
                oT = spike
                U = drive[:, :, :].rearrange("p a (b v) -> p (a b) v", v=64)
                R = al[:, :, :].rearrange("p a (b v) -> p (a b) v", v=64)
                V = kq[:, 0, :, :].rearrange("p a (b v) -> p (a b) v", v=64)
                PT = kr[:, :, :].rearrange("p a (b v) -> p (a b) v", v=64)

                def wide(t, bk, n=32):
                    return t[:, bk * PB:(bk + 1) * PB, :]

                def level(l):
                    return lm[:, l, :].unsqueeze(1).to_broadcast([128, PB, 32])

                def units(hp):
                    for b in range(GB):
                        yield hp * GB + b, b

                @block.tensor
                def _(pe):
                    ln_pe(pe, s, xg[:, :])
                    pe.wait_ge(s["ln_out"], 1)
                    ln_pe(pe, s, z[:, :], n=2, rms=True)
                    pe.wait_ge(s["h"], 1)
                    pe.matmul(bank[6][0:64, :], col("wau", 0, 64), h[:, :], start=True, stop=True).then_inc(s["au_ps"], 1)
                    for j in range(16):
                        kind, m = divmod(j, 4)
                        if 4 <= j < 8:
                            pe.wait_ge(s["drive_read"], j - 3)
                        elif j >= 8:
                            pe.wait_ge(s["proj_read"], j - 7)
                        if kind == 3:
                            pe.wait_ge(s["au"], 1)
                            lhsT, rhs = wD[0:64, 4, m * 128:(m + 1) * 128], au[:, :]
                        else:
                            lhsT, rhs = wD[:, (3, 0, 1)[kind], m * 128:(m + 1) * 128], h[:, :]
                        pe.matmul(bank[j % 4][:, :], lhsT, rhs, start=True, stop=True).then_inc(s["proj"], 1)
                    for n in range(8):
                        pe.wait_ge(s["squared"], n + 1)
                        pe.matmul(bank[4][0:16, :], col("norm_rows", 16 * n, 16), tmp[:, n % 2, :], start=n == 0,
                                  stop=n == 7).then_inc(s["norm_ps"], 1)
                    pe.matmul(bank[7][0:64, :], col("wu1", 0, 64), z[:, :], start=True, stop=True).then_inc(s["g1_ps"], 1)
                    pe.wait_ge(s["g1"], 1)
                    pe.matmul(bank[7][:, :], col("wu2", 0, 128, p=64), au[:, :], start=True, stop=True).then_inc(s["g2_ps"], 1)

                    def spiked(j):
                        if j >= 2:
                            pe.wait_ge(s["kr"], j - 1)
                        pe.matmul(bank[4 + j % 2][:, :], BLOCKSUM, spike[:, j, :], start=True, stop=True)\
                            .then_inc(s["count"], 1)
                        pe.matmul(bank[6 + j % 2][:, :], wD[:, 5, j * 128:(j + 1) * 128], h[:, :], start=True, stop=False)
                        pe.matmul(bank[6 + j % 2][:, :], wD[:, 6, j * 128:(j + 1) * 128], spike[:, j, :], start=False,
                                  stop=True).then_inc(s["beta_ps"], 1)

                    pe.wait_ge(s["norm_root"], 1)
                    pe.wait_ge(s["g2"], 1)
                    for j in range(2):
                        pe.wait_ge(s["spikes"], j + 1)
                        spiked(j)
                    pe.wait_ge(s["proj_read"], 12)
                    pe.wait_ge(s["norm"], 1)
                    for i, n in enumerate(NORM_ORDER):
                        if i >= 4:
                            pe.wait_ge(s["normed"], i - 3)
                        pe.matmul(bank[i % 4][:, :], nsel[:, n, :], nrm[:, :], start=True, stop=True)\
                            .then_inc(s["norm_bc"], 1)
                    for j in range(2, HDP):
                        pe.wait_ge(s["spikes"], j + 1)
                        spiked(j)
                    pe.wait_ge(s["normed"], 8)
                    pe.wait_ge(s["kr"], HDP)
                    def per_quadrant(hp, out, cols, lhsT, rhs):
                        for u, b in units(hp):
                            for q in range(4):
                                r, t0 = slice(64 * (q // 2), 64 * (q // 2) + 64), b * S + 32 * (q % 2)
                                last = pe.matmul(out[32 * q:32 * q + 32, b * cols:(b + 1) * cols], lhsT(r, t0), rhs(r, t0),
                                                 start=b == 0, stop=True, skip_group_check=True)
                        return last

                    for hp in range(HDP):
                        per_quadrant(hp, bank[hp], 32, lambda r, t0: kr[r, hp, t0:t0 + 32],
                                     lambda r, t0: kq[r, 1, hp, t0:t0 + 32]).then_inc(s["diag_ps"], 1)

                    def products(l):
                        for hp in range(HDP):
                            pe.wait_ge(s["scaled_kq"], HDP * l + hp + 1)
                            if l > 0:
                                pe.wait_ge(s["scaled_kr"], HDP * (l - 1) + hp + 1)
                                pe.wait_ge(s["masked"], HDP * (l - 1) + hp + 1)
                            else:
                                pe.wait_ge(s["diag"], hp + 1)
                            if l < len(LEVELS):
                                last = per_quadrant(hp, bank[hp], 64, lambda r, t0: kr[r, hp, t0:t0 + 32],
                                                    lambda r, t0: kq[r, :, hp, t0:t0 + 32])
                            else:
                                for u, b in units(hp):
                                    for par in range(2):
                                        r = slice(64 * par, 64 * par + 64)
                                        last = pe.matmul(bank[hp][64 * par:64 * par + 32, b * 64:(b + 1) * 64],
                                                         kr[r, hp, b * S:b * S + 32], kq[r, :, hp, b * S + 32:b * S + 64],
                                                         start=b == 0, stop=True, skip_group_check=True)
                            last.then_inc(s["products"], 1)

                    def blockwise(hp, at, lhsT, rhs):
                        for u, b in units(hp):
                            for q in range(4):
                                r = slice(32 * q, 32 * q + 32)
                                last = pe.matmul(bank[4 + hp][r, at + b * 32:at + (b + 1) * 32], lhsT[r, u, :], rhs[r, u, :],
                                                 start=b == 0, stop=True, skip_group_check=True)
                        return last

                    products(0)
                    products(1)
                    for l in range(1, len(LEVELS)):
                        for hp in range(HDP):
                            pe.wait_ge(s["masked"], HDP * l + hp + 1)
                            pe.wait_ge(s["inverse"], HDP * (l - 1) + hp + 1)
                            blockwise(hp, 0, aT, X).then_inc(s["w_ps"], 1)
                        products(l + 1)
                        for hp in range(HDP):
                            pe.wait_ge(s["w"], HDP * (l - 1) + hp + 1)
                            blockwise(hp, 256, XT, W).then_inc(s["xw_ps"], 1)
                    pe.wait_ge(s["inverse"], HDP * len(LEVELS))
                    for b in range(GB):
                        for par in range(2):
                            last = pe.matmul(bank[4 + b // 2][64 * par:64 * par + 64, (b % 2) * 256:(b % 2) * 256 + 256],
                                             h[:, b * S:(b + 1) * S], wD[:, 2, par * 256:(par + 1) * 256],
                                             start=b % 2 == 0, stop=True, skip_group_check=True)
                    last.then_inc(s["v_ps"], 1)
                    pe.wait_ge(s["v"], 1)
                    for hp in range(HDP):
                        pe.wait_ge(s["joined"], hp + 1)
                        for u, b in units(hp):
                            for q in range(4):
                                r = slice(32 * q, 32 * q + 32)
                                last = pe.matmul(bank[hp][r, b * 64:(b + 1) * 64], XT[r, u, :], V[r, u, :],
                                                 start=b == 0, stop=True, skip_group_check=True)
                        last.then_inc(s["y_ps"], 1)
                    for hp in range(HDP):
                        pe.wait_ge(s["y"], hp + 1)
                        for u, b in units(hp):
                            for par in range(2):
                                r, r2 = slice(64 * par, 64 * par + 32), slice(64 * par + 32, 64 * par + 64)
                                last = pe.matmul(bank[4 + hp][r2, b * 64:(b + 1) * 64], aT[r, u, :], U[r, u, :],
                                                 start=b == 0, stop=True, skip_group_check=True)
                        last.then_inc(s["r_ps"], 1)
                    for hp in range(HDP):
                        pe.wait_ge(s["r"], hp + 1)
                        for u, b in units(hp):
                            for par in range(2):
                                r2 = slice(64 * par + 32, 64 * par + 64)
                                last = pe.matmul(bank[hp][r2, b * 64:(b + 1) * 64], XT[r2, u, :], R[r2, u, :],
                                                 start=b == 0, stop=True, skip_group_check=True)
                        last.then_inc(s["u2_ps"], 1)
                    for hp in range(HDP):
                        pe.wait_ge(s["u"], hp + 1)
                        for u, b in units(hp):
                            for par in range(2):
                                r = slice(64 * par, 64 * par + 64)
                                last = pe.matmul(bank[4 + hp][r, b * S:(b + 1) * S], U[r, u, :], PT[r, u, :], start=b == 0,
                                                 stop=True, skip_group_check=True)
                        last.then_inc(s["o_ps"], 1)
                    for n in range(HDP):
                        pe.wait_ge(s["o_squared"], n + 1)
                        pe.matmul(bank[2][0:8, :], col("norm_rows", 16 * n, 8), tmp[:, n % 2, :], start=n == 0,
                                  stop=n == HDP - 1).then_inc(s["o_norm_ps"], 1)
                    pe.wait_ge(s["o_norm"], 1)
                    for n in range(HDP):
                        if n >= 2:
                            pe.wait_ge(s["o"], n - 1)
                        pe.matmul(bank[n % 2][:, :], nsel[0:8, n, :], nrm[0:8, :], start=True, stop=True)\
                            .then_inc(s["o_norm_bc"], 1)
                    pe.wait_ge(s["o"], HDP)
                    for n in range(HDP):
                        last = pe.matmul(bank[2][:, :], wD[:, 7, n * 128:(n + 1) * 128], oT[:, n, :], start=n == 0,
                                         stop=n == HDP - 1)
                    last.then_inc(s["wo_ps"], 1)
                    pe.wait_ge(s["y2"], 1)
                    ln_pe(pe, s, h[:, :], n=3, rms=True)
                    pe.wait_ge(s["zz"], 1)
                    for n in range(4):
                        if n >= 2:
                            pe.wait_ge(s["ff"], n - 1)
                        pe.matmul(bank[2 + n % 2][:, :], wD[:, 8, n * 128:(n + 1) * 128], z[:, :], start=True, stop=True)
                        pe.matmul(bank[4 + n % 2][:, :], wD[:, 9, n * 128:(n + 1) * 128], z[:, :], start=True, stop=True)\
                            .then_inc(s["ff_ps"], 1)
                    for n in range(4):
                        pe.wait_ge(s["ff"], n + 1)
                        last = pe.matmul(bank[6][:, :], wD[:, 10, n * 128:(n + 1) * 128], drive[:, n, :], start=n == 0,
                                         stop=n == 3)
                    last.then_inc(s["down"], 1)

                @block.scalar
                def _(act):
                    ln_act(act, s)
                    act.wait_ge(s["ln_out"], 1)
                    ln_act(act, s, src=z[:, :], n=2, rms=True, eps=RMS_EPS, then=ACT.Silu)
                    act.wait_ge(s["conv"], 1)
                    act.activation(h[:, :], tmp[:, 0, :], ACT.Silu, bias=col("conv_b")).then_inc(s["h"], 1)
                    act.wait_ge(s["au_ps"], 1)
                    act.activation(au[:, :], bank[6][0:64, :], ACT.Silu, bias=col("bau", p=64)).then_inc(s["au"], 1)

                    for j in range(4, 16):
                        kind, m = divmod(j, 4)
                        dst = (None, kq[:, 1, m, :], kq[:, 0, m, :], al[:, m, :])[kind]
                        act.wait_ge(s["proj"], j + 1)
                        act.activation(dst, bank[j % 4][:, :], ACT.Copy).then_inc(s["proj_read"], 1)
                    for n in range(8):
                        act.wait_ge(s["proj_read"], n + 1)
                        if n >= 2:
                            act.wait_ge(s["norm_ps"], n - 1)
                        if n == 0:
                            act.wait_ge(s["h"], 1)
                        act.activation(tmp[:, n % 2, :], kq[:, (n // 4 + 1) % 2, n % 4, :], ACT.Square).then_inc(s["squared"], 1)
                    act.wait_ge(s["norm_ps"], 8)
                    act.activation(nrm[:, :], bank[4][0:16, :], ACT.Sqrt).then_inc(s["norm_root"], 1)
                    act.wait_ge(s["g1_ps"], 1)
                    act.activation(au[:, :], bank[7][0:64, :], ACT.Silu, bias=col("bu1", p=64)).then_inc(s["g1"], 1)
                    act.wait_ge(s["g2_ps"], 1)
                    act.activation(gate[:, :], bank[7][:, :], ACT.Sigmoid, bias=col("bu2")).then_inc(s["g2"], 1)
                    for j in range(HDP):
                        act.wait_ge(s["alpha_pre"], j + 1)
                        act.activation(al[:, j, :], al[:, j, :], ACT.Sigmoid, bias=col("bad", j)).then_inc(s["alpha"], 1)
                        act.wait_ge(s["beta_ps"], j + 1)
                        if j >= 2:
                            act.wait_ge(s["kr"], j - 1)
                        act.activation(nb[:, j % 2, :], bank[6 + j % 2][:, :], ACT.Sigmoid, bias=col("bbeta", j))\
                            .then_inc(s["beta"], 1)
                    for l in range(1, len(LEVELS)):
                        for hp in range(HDP):
                            act.wait_ge(s["w_ps"], HDP * (l - 1) + hp + 1)
                            act.activation(wide(W, hp), bank[4 + hp][:, 0:256].rearrange("p (u n) -> p u n", n=32), ACT.Copy)\
                                .then_inc(s["w"], 1)
                    act.preload_act_table_set("natural_log_exp_and_others")
                    act.wait_ge(s["products"], HDP * (len(LEVELS) + 1))
                    act.wait_ge(s["masked"], HDP * len(LEVELS))
                    act.wait_ge(s["zeros"], 1)
                    for hp in range(HDP):
                        for par in range(2):
                            r = slice(64 * par, 64 * par + 32)
                            last = act.activation(
                                PT[r, hp * PB:(hp + 1) * PB, 32:64],
                                bank[hp][r, :].rearrange("p (u n) -> p u n", n=64)[:, :, 32:64], ACT.Copy)
                        last.then_inc(s["p_join"], 1)
                    for q in range(4):
                        r = slice(32 * q, 32 * q + 32)
                        act.activation(PT[r, :, 32 * (q % 2):32 * (q % 2) + 32], pc[r, :, :], ACT.Copy)\
                            .then_inc(s["p_t"], 1)
                    act.wait_ge(s["v_ps"], 1)
                    for bk in range(4):
                        last = act.activation(
                            V.rearrange("p (h b) v -> p b h v", h=HDP)[:, 2 * bk:2 * bk + 2, :, :],
                            bank[4 + bk][:, :].rearrange("p (b h v) -> p b h v", b=2, h=HDP), ACT.Copy)
                    last.then_inc(s["v"], 1)
                    for hp in range(HDP):
                        act.wait_ge(s["r_ps"], hp + 1)
                        for par in range(2):
                            r2 = slice(64 * par + 32, 64 * par + 64)
                            last = act.activation(R[r2, hp * PB:(hp + 1) * PB, :],
                                                  bank[4 + hp][r2, :].rearrange("p (u n) -> p u n", n=64), ACT.Copy)
                        last.then_inc(s["r"], 1)
                    for n in range(HDP):
                        act.wait_ge(s["o_ps"], n + 1)
                        if n >= 2:
                            act.wait_ge(s["o_norm_ps"], n - 1)
                        act.activation(tmp[:, n % 2, :], bank[4 + n][:, :], ACT.Square).then_inc(s["o_squared"], 1)
                    act.wait_ge(s["o_norm_ps"], HDP)
                    act.activation(nrm[0:8, :], bank[2][0:8, :], ACT.Ln, bias=eps_tiles[RMS_EPS][0:8, :], scale=1.0 / 64)\
                        .then_inc(s["o_norm_log"], 1)
                    act.wait_ge(s["o_norm_log"], 1)
                    act.activation(nrm[0:8, :], nrm[0:8, :], ACT.Exp, scale=-0.5).then_inc(s["o_norm"], 1)
                    act.wait_ge(s["y2"], 1)
                    ln_act(act, s, src=h[:, :], n=3, rms=True, eps=RMS_EPS, then=ACT.Silu)
                    for n in range(4):
                        act.wait_ge(s["ff_ps"], n + 1)
                        if n >= 2:
                            act.wait_ge(s["ff"], n - 1)
                        act.activation(tmp[:, n % 2, :], bank[2 + n % 2][:, :], ACT.Silu).then_inc(s["ff_silu"], 1)

                @block.gpsimd
                def _(pool):
                    pool.memset(hc[:, :, 0:3], 0.0).then_inc(s["pad"], 1)

                    def halves(t, c):
                        return t.rearrange("p (m two c) -> p m two c", two=2, c=c)

                    for l, c in enumerate(LEVELS):
                        for hp in range(HDP):
                            pool.wait_ge(s["products"], HDP * l + hp + 1)
                            pool.wait_ge(s["scaled_kq"], HDP * (l + 1) + hp + 1)
                            if l > 0:
                                pool.wait_ge(s["scaled_kr"], HDP * (l - 1) + hp + 1)
                            r_, a_ = halves(kr[:, hp, :], c), halves(al[:, hp, :], c)
                            pool.tensor_tensor(r_[:, :, 0, :], r_[:, :, 0, :],
                                               a_[:, :, 1, 0:1].to_broadcast([128, T // (2 * c), c]), ALU.mult)
                            pool.tensor_tensor(a_[:, :, 0, 0:1], a_[:, :, 0, 0:1], a_[:, :, 1, 0:1], ALU.mult)\
                                .then_inc(s["scaled_kr"], 1)
                    pool.wait_ge(s["products"], HDP * (len(LEVELS) + 1))
                    for par in range(2):
                        last = pool.memset(PT[64 * par + 32:64 * par + 64, :, 0:32], 0.0)
                    last.then_inc(s["zeros"], 1)

                @block.vector
                def _(dve):
                    link = link_of(dve, s["dve"])
                    ln_dve(dve, s, xg[:, :], z[:, :])
                    ln_reciprocal(dve, s, 2)
                    dve.wait_ge(s["ln_rstd"], nth(2, 1))
                    dve.wait_ge(s["ln_out"], 1)
                    dve.wait_ge(s["pad"], 1)

                    def tok(t):
                        return t.rearrange("p (b t) -> p b t", t=S)
                    link(dve.scalar_tensor_tensor(hc[:, :, 3:3 + S], tok(z[:, :]), col("norm_in"), tok(rs[:, :]), ALU.mult,
                                                  ALU.mult))
                    cv = tok(tmp[:, 0, :])
                    link(dve.tensor_scalar(cv, hc[:, :, 0:S], col("conv_w", 0), None, ALU.mult))
                    for i in range(1, 4):
                        last = dve.scalar_tensor_tensor(cv, hc[:, :, i:i + S], col("conv_w", i), cv, ALU.mult, ALU.add)
                        if i < 3:
                            link(last)
                    last.then_inc(s["conv"], 1)
                    for j in range(HDP):
                        dve.wait_ge(s["proj"], j + 1)
                        dve.tensor_scalar(drive[:, j, :], bank[j][:, :], 2.0, None, ALU.mult).then_inc(s["drive_read"], 1)
                    dve.wait_ge(s["drive_read"], HDP)
                    dr = drive[:, :, :].rearrange("p h (b t) -> p h b t", t=S)
                    for t in range(S):
                        m_ = dr[:, :, :, t]
                        if t >= 1:
                            last = dve.scalar_tensor_tensor(m_, mem[:, :, :], -0.9, m_, ALU.mult, ALU.add)
                            link(last)
                        if t < S - 1:
                            link(dve.scalar_tensor_tensor(mem[:, :, :], m_, 1.0, m_, ALU.is_gt, ALU.subtract))
                    for j in range(HDP):
                        dve.tensor_scalar(spike[:, j, :], drive[:, j, :], 1.0, None, ALU.is_gt).then_inc(s["spikes"], 1)
                    for j in range(HDP):
                        dve.wait_ge(s["spikes"], j + 1)
                        dve.wait_ge(s["proj_read"], 8 + j + 1)
                        dve.scalar_tensor_tensor(al[:, j, :], spike[:, j, :], col("asp", j), al[:, j, :], ALU.mult, ALU.add)\
                            .then_inc(s["alpha_pre"], 1)
                    dve.wait_ge(s["norm_root"], 1)
                    link(dve.tensor_scalar(nrm[:, :], nrm[:, :], 1e-6, None, ALU.add))
                    dve.reciprocal(nrm[:, :], nrm[:, :]).then_inc(s["norm"], 1)

                    def normalize(i):
                        n = NORM_ORDER[i]
                        dve.wait_ge(s["norm_bc"], i + 1)
                        x_ = kq[:, (n // 4 + 1) % 2, n % 4, :]
                        dve.tensor_tensor(x_, x_, bank[i % 4][:, :], ALU.mult).then_inc(s["normed"], 1)

                    for i in range(4):
                        normalize(i)
                    for j in range(HDP):
                        if j == 2:
                            for i in range(4, 8):
                                normalize(i)
                        dve.wait_ge(s["normed"], j + 1)
                        dve.wait_ge(s["count"], j + 1)
                        dve.wait_ge(s["alpha"], j + 1)
                        dve.scalar_tensor_tensor(al[:, j, :], bank[4 + j % 2][:, :], 0.0, al[:, j, :], ALU.is_equal, ALU.max)
                        dve.wait_ge(s["beta"], j + 1)
                        link(dve.scalar_tensor_tensor(nb[:, j % 2, :], bank[4 + j % 2][:, :], 0.0, nb[:, j % 2, :], ALU.is_gt,
                                                      ALU.mult))
                        dve.tensor_tensor(kr[:, j, :], kq[:, 0, j, :], nb[:, j % 2, :], ALU.mult).then_inc(s["kr"], 1)
                    for hp in range(HDP):
                        dve.wait_ge(s["diag_ps"], hp + 1)
                        dve.tensor_tensor(wide(pc, hp), bank[hp][:, 0:256].rearrange("p (u n) -> p u n", n=32), level(5),
                                          ALU.mult).then_inc(s["diag"], 1)
                    for hp in range(HDP):
                        both = kq[:, :, hp, :]
                        dve.tensor_tensor(both, both, al[:, hp:hp + 1, :].to_broadcast([128, 2, T]), ALU.mult)\
                            .then_inc(s["scaled_kq"], 1)

                    def mask(l, c):
                        for hp in range(HDP):
                            dve.wait_ge(s["products"], HDP * l + hp + 1)
                            if l == 0:
                                dve.wait_ge(s["diag"], hp + 1)
                            if l >= 2:
                                dve.wait_ge(s["w_ps"], HDP * (l - 2) + hp + 1)
                            ps = bank[hp][:, :].rearrange("p (u n) -> p u n", n=64)
                            dve.tensor_tensor(wide(aT, hp), ps[:, :, 0:32], level(l), ALU.mult)
                            dve.copy_predicated(wide(pc, hp), lmi[:, l, :].unsqueeze(1).to_broadcast([128, PB, 32]),
                                                ps[:, :, 32:64]).then_inc(s["masked"], 1)
                            dve.wait_ge(s["scaled_kq"], HDP * l + hp + 1)
                            if l > 0:
                                dve.wait_ge(s["scaled_kr"], HDP * (l - 1) + hp + 1)
                            v = kq[:, :, hp, :].rearrange("p i (m two c) -> p i m two c", two=2, c=c)[:, :, :, 1, :]
                            f = al[:, hp, :].rearrange("p (m two c) -> p m two c", two=2, c=c)[:, :, 0, 0:1]
                            m = T // (2 * c)
                            if c == 1:
                                v = v.rearrange("p i m c -> p i (m c)")
                                f = f.rearrange("p m c -> p (m c)").unsqueeze(1).to_broadcast([128, 2, m])
                                dve.tensor_tensor(v, v, f, ALU.mult).then_inc(s["scaled_kq"], 1)
                            else:
                                dve.tensor_tensor(v, v, f.unsqueeze(1).to_broadcast([128, 2, m, c]), ALU.mult)\
                                    .then_inc(s["scaled_kq"], 1)

                    mask(0, LEVELS[0])
                    for hp in range(HDP):
                        dve.wait_ge(s["masked"], hp + 1)
                        link(dve.tensor_tensor(wide(XT, hp), level(5), wide(aT, hp), ALU.subtract))
                        dve.transpose(wide(X, hp).rearrange("p u n -> p (u n)"), wide(XT, hp).rearrange("p u n -> p (u n)"))\
                            .then_inc(s["inverse"], 1)
                    mask(1, LEVELS[1])
                    for l in range(1, len(LEVELS)):
                        if l + 1 < len(LEVELS):
                            mask(l + 1, LEVELS[l + 1])
                        for hp in range(HDP):
                            dve.wait_ge(s["xw_ps"], HDP * (l - 1) + hp + 1)
                            link(dve.tensor_tensor(wide(X, hp), wide(X, hp),
                                                   bank[4 + hp][:, 256:512].rearrange("p (u n) -> p u n", n=32), ALU.subtract))
                            dve.transpose(wide(XT, hp).rearrange("p u n -> p (u n)"),
                                          wide(X, hp).rearrange("p u n -> p (u n)")).then_inc(s["inverse"], 1)
                    for hp in range(HDP):
                        dve.wait_ge(s["p_join"], hp + 1)
                        for par in range(2):
                            r = slice(64 * par, 64 * par + 32)
                            last = dve.tensor_copy(aT[r, hp * PB:(hp + 1) * PB, :],
                                                   bank[hp][r, :].rearrange("p (u n) -> p u n", n=64)[:, :, 0:32])
                        last.then_inc(s["joined"], 1)
                    for hp in range(HDP):
                        dve.wait_ge(s["y_ps"], hp + 1)
                        dve.tensor_copy(wide(U, hp), bank[hp][:, :].rearrange("p (u n) -> p u n", n=64)).then_inc(s["y"], 1)
                    for hp in range(HDP):
                        dve.wait_ge(s["y"], hp + 1)
                        dve.wait_ge(s["u2_ps"], hp + 1)
                        if hp == 0:
                            dve.wait_ge(s["p_t"], 4)
                        for par in range(2):
                            r2 = slice(64 * par + 32, 64 * par + 64)
                            u_ = U[r2, hp * PB:(hp + 1) * PB, :]
                            last = dve.tensor_tensor(u_, u_, bank[hp][r2, :].rearrange("p (u n) -> p u n", n=64),
                                                     ALU.subtract)
                        last.then_inc(s["u"], 1)
                    for n in range(HDP):
                        dve.wait_ge(s["o_norm_bc"], n + 1)
                        link(dve.tensor_copy(nb[:, n % 2, :], bank[n % 2][:, :]))
                        dve.scalar_tensor_tensor(oT[:, n, :], bank[4 + n][:, :], col("headw", n), nb[:, n % 2, :], ALU.mult,
                                                 ALU.mult).then_inc(s["o"], 1)
                    dve.wait_ge(s["wo_ps"], 1)
                    dve.wait_ge(s["g2"], 1)
                    link(dve.tensor_tensor(h[:, :], gate[:, :], bank[2][:, :], ALU.mult))
                    dve.tensor_tensor(h[:, :], h[:, :], z[:, :], ALU.add).then_inc(s["y2"], 1)
                    ln_reciprocal(dve, s, 3)
                    dve.wait_ge(s["ln_rstd"], nth(3, 1))
                    dve.wait_ge(s["y2"], 1)
                    dve.scalar_tensor_tensor(z[:, :], h[:, :], col("ffw"), rs[:, :], ALU.mult, ALU.mult).then_inc(s["zz"], 1)
                    for n in range(4):
                        dve.wait_ge(s["ff_silu"], n + 1)
                        dve.tensor_tensor(drive[:, n, :], tmp[:, n % 2, :], bank[4 + n % 2][:, :], ALU.mult)\
                            .then_inc(s["ff"], 1)
                    link(dve.tensor_tensor(xg[:, :], xg[:, :], h[:, :], ALU.add))
                    dve.wait_ge(s["down"], 1)
                    dve.tensor_tensor(xg[:, :], xg[:, :], bank[6][:, :], ALU.add)

            run_stage("delta", LN + "h au_ps au proj drive_read proj_read squared norm_ps norm_root norm norm_bc normed pad conv spikes count "
                           "alpha_pre alpha beta_ps beta kr diag_ps diag scaled_kq scaled_kr products masked inverse w_ps "
                           "w xw_ps joined zeros p_join p_t v_ps v y_ps y r_ps r u2_ps u o_ps o_squared o_norm_ps "
                           "o_norm_log o_norm o_norm_bc o g1_ps g1 g2_ps g2 wo_ps y2 zz ff_ps ff_silu ff down dve", body)

        def mlstm(g):
            NB = NHX * NP
            isq = 1.0 / float(np.sqrt(np.float32(DHX)))

            def body(ctx, s, block):
                keep_rows = sb("keep_rows", [NHX, T], ctx=ctx)
                drop_rows = sb("drop_rows", [NHX, T], ctx=ctx)
                f = sb("f_gate", [NHX, T], ctx=ctx)
                lf = sb("log_f", [NHX, T], ctx=ctx)
                cs = sb("cumulated", [NHX, T], ctx=ctx)
                a = sb("gate_a", [NHX, T], ctx=ctx)
                M = sb("running_max", [NHX, T], ctx=ctx)
                m2 = sb("neg_max_log", [NHX, T], ctx=ctx)
                aT = sb("gate_a_t", [128, NP, NHX], ctx=ctx)
                em = sb("exp_neg_max", [128, NP, NHX], ctx=ctx)
                dm = sb("decay", [128, NHX, NP, S], ctx=ctx)
                cT = sb("weights_t", [128, NHX, NP, S], ctx=ctx)
                nrm = sb("normalizer", [128, NP, NHX], ctx=ctx)
                hn = sb("head_out", [128, NP, NHX, DHX], ctx=ctx)
                hq = sb("head_sq", [128, NP, NHX, DHX], ctx=ctx)
                st = sb("head_stat", [128, NP, NHX], ctx=ctx)

                @block.tensor
                def _(pe):
                    ln_pe(pe, s, xg[:, :])
                    pe.wait_ge(s["ln_out"], 1)
                    for gate in range(2):
                        for part in range(3):
                            last = pe.matmul(bank[2 + gate][0:NHX, :],
                                             col("gates", part * 2 * NHX + gate * NHX, NHX), (z if part == 0 else cg)[:, :],
                                             start=part == 0, stop=part == 2)
                    last.then_inc(s["gates"], 1)
                    for h in range(NHX):
                        for b in range(GB):
                            bp, par = divmod(b, 2)
                            last = pe.matmul(bank[4 + h][64 * par:64 * par + 64, bp * S:(bp + 1) * S],
                                             cg[32 * h:32 * h + 32, b * S:(b + 1) * S], z[32 * h:32 * h + 32, b * S:(b + 1) * S],
                                             start=bp == 0, stop=True, skip_group_check=True)
                    last.then_inc(s["qk"], 1)
                    pe.wait_ge(s["rows"], 1)
                    for i, row in enumerate((a, m2)):
                        for bp in range(NP):
                            at = bp * NHX
                            last = pe.transpose(bank[i][:, at:at + NHX], row[:, bp * 128:(bp + 1) * 128],
                                                cst[0:NHX, 2, 0:NHX])
                    last.then_inc(s["columns"], 1)
                    for half in range(2):
                        pe.matmul(bank[2 + half][:, :], identb[:, :], cmT[:, :], start=True, stop=False,
                                  skip_group_check=True)
                        for i in range(2):
                            h = 2 * half + i
                            for par in range(2):
                                rhs = M[:, :].rearrange("p (b c s) -> p b c s", c=2, s=S)[:, :, par, :]
                                last = pe.matmul(bank[2 + half][64 * par:64 * par + 64, i * 256:(i + 1) * 256],
                                                 self_[0:NHX, h, 0:64], rhs, start=False, stop=True,
                                                 skip_group_check=True)
                    last.then_inc(s["neg_max"], 1)
                    pe.wait_ge(s["weights"], NHX)
                    for b in range(GB):
                        bp, par = divmod(b, 2)
                        for h in range(NHX):
                            at = ((bp % 2) * NHX + h) * (DHX + 1)
                            last = pe.matmul(bank[2 + bp // 2][64 * par:64 * par + 64, at:at + DHX + 1],
                                             cT[64 * par:64 * par + 64, h, bp, :], ctk[64 * par:64 * par + 64, bp, h, :],
                                             start=bp % 2 == 0 and h == 0, stop=True, skip_group_check=True)
                    last.then_inc(s["attended"], 1)
                    pe.wait_ge(s["head_out"], 1)
                    for bp in range(NP):
                        last = pe.transpose(bank[1][:, bp * 128:(bp + 1) * 128],
                                            hn[:, bp, :, :].rearrange("p h d -> p (h d)"), IDENT)
                    last.then_inc(s["out_t"], 1)

                @block.gpsimd
                def _(pool):
                    pool.memset(keep_rows[:, :], 1.0)
                    pool.memset(drop_rows[:, :], 0.0).then_inc(s["rows_set"], 1)
                    pool.wait_ge(s["rows_set"], 1)
                    pool.memset(keep_rows[:, 0:T:S], 0.0)
                    pool.memset(drop_rows[:, 0:T:S], NEG).then_inc(s["rows_set"], 1)

                @block.scalar
                def _(act):
                    link = link_of(act, s["act"])
                    ln_act(act, s)
                    act.preload_act_table_set("natural_log_exp_and_others")
                    act.wait_ge(s["f"], 1)
                    link(act.activation(lf[:, :], f[:, :], ACT.Abs))
                    link(act.activation(lf[:, :], lf[:, :], ACT.Exp, scale=-1.0))
                    act.activation(lf[:, :], lf[:, :], ACT.Ln, bias=1.0).then_inc(s["log"], 1)
                    act.wait_ge(s["columns"], 1)
                    act.activation(em[:, :, :], bank[1][:, 0:NB].rearrange("p (b h) -> p b h", h=NHX), ACT.Exp)\
                        .then_inc(s["exp_max"], 1)
                    for half in range(2):
                        act.wait_ge(s["log_decay"], half + 1)
                        act.activation(dm[:, 2 * half:2 * half + 2, :, :], dm[:, 2 * half:2 * half + 2, :, :], ACT.Exp)\
                            .then_inc(s["decay"], 1)
                    act.wait_ge(s["head_var"], 1)
                    link(act.activation(st[:, :, :], st[:, :, :], ACT.Ln, bias=eps_tiles[LN_EPS], scale=1.0 / DHX))
                    act.activation(st[:, :, :], st[:, :, :], ACT.Exp, scale=-0.5).then_inc(s["head_std"], 1)

                @block.vector
                def _(dve):
                    link = link_of(dve, s["dve"])

                    def bc(t, n=DHX):
                        return t.unsqueeze(3).to_broadcast([128, NP, NHX, n])

                    ln_dve(dve, s, xg[:, :], z[:, :])
                    dve.wait_ge(s["gates"], 1)
                    dve.tensor_scalar(f[:, :], bank[3][0:NHX, :], col("gfb", p=NHX), None, ALU.add).then_inc(s["f"], 1)
                    dve.wait_ge(s["log"], 1)
                    link(dve.scalar_tensor_tensor(lf[:, :], f[:, :], 0.0, lf[:, :], ALU.min, ALU.subtract))
                    dve.wait_ge(s["rows_set"], 2)
                    link(dve.tensor_tensor_scan(cs[:, :], keep_rows[:, :], lf[:, :], 0.0, ALU.mult, ALU.add))
                    link(dve.scalar_tensor_tensor(a[:, :], bank[2][0:NHX, :], col("gib", p=NHX), cs[:, :], ALU.add,
                                                  ALU.subtract))
                    link(dve.tensor_tensor_scan(M[:, :], drop_rows[:, :], a[:, :], 0.0, ALU.add, ALU.max))
                    link(dve.scalar_tensor_tensor(m2[:, :], cs[:, :], -1.0, M[:, :], ALU.mult, ALU.subtract))
                    dve.tensor_scalar(M[:, :], M[:, :], -1.0, None, ALU.mult).then_inc(s["rows"], 1)
                    dve.wait_ge(s["columns"], 1)
                    link(dve.tensor_copy(aT[:, :, :], bank[0][:, 0:NB].rearrange("p (b h) -> p b h", h=NHX)))
                    dve.wait_ge(s["neg_max"], 1)
                    for half in range(2):
                        for i in range(2):
                            h = 2 * half + i
                            last = dve.tensor_tensor(
                                dm[:, h, :, :], bank[2 + half][:, i * 256:(i + 1) * 256].rearrange("p (b s) -> p b s", s=S),
                                aT[:, :, h:h + 1].to_broadcast([128, NP, S]), ALU.add)
                        last.then_inc(s["log_decay"], 1)
                    dve.wait_ge(s["qk"], 1)
                    for h in range(NHX):
                        dve.wait_ge(s["decay"], h // 2 + 1)
                        dve.scalar_tensor_tensor(cT[:, h, :, :], bank[4 + h][:, 0:256].rearrange("p (b s) -> p b s", s=S),
                                                 isq, dm[:, h, :, :], ALU.mult, ALU.mult).then_inc(s["weights"], 1)
                    dve.wait_ge(s["attended"], 1)

                    def attended(i, c0, c1):
                        return bank[2 + i][:, 0:2 * NHX * (DHX + 1)].rearrange("p (b h d) -> p b h d", b=2, d=DHX + 1)[:, :, :, c0:c1]
                    for i in range(2):
                        last = dve.tensor_copy(nrm[:, 2 * i:2 * i + 2, :].unsqueeze(3), attended(i, DHX, DHX + 1))
                    link(last)
                    link(dve.scalar_tensor_tensor(nrm[:, :, :], nrm[:, :, :], -1.0, nrm[:, :, :], ALU.mult, ALU.max))
                    dve.wait_ge(s["exp_max"], 1)
                    link(dve.tensor_tensor(nrm[:, :, :], nrm[:, :, :], em[:, :, :], ALU.max))
                    link(dve.tensor_scalar(nrm[:, :, :], nrm[:, :, :], 1e-6, None, ALU.add))
                    link(dve.reciprocal(nrm[:, :, :], nrm[:, :, :]))
                    for i in range(2):
                        last = dve.tensor_tensor(hn[:, 2 * i:2 * i + 2, :, :], attended(i, 0, DHX),
                                                 nrm[:, 2 * i:2 * i + 2, :].unsqueeze(3).to_broadcast([128, 2, NHX, DHX]),
                                                 ALU.mult)
                    link(last)
                    link(dve.tensor_reduce(st[:, :, :], hn[:, :, :, :], AX, ALU.add))
                    link(dve.tensor_scalar(st[:, :, :], st[:, :, :], 1.0 / DHX, None, ALU.mult))
                    link(dve.tensor_tensor(hn[:, :, :, :], hn[:, :, :, :], bc(st[:, :, :]), ALU.subtract))
                    link(dve.tensor_tensor(hq[:, :, :, :], hn[:, :, :, :], hn[:, :, :, :], ALU.mult))
                    dve.tensor_reduce(st[:, :, :], hq[:, :, :, :], AX, ALU.add).then_inc(s["head_var"], 1)
                    dve.wait_ge(s["head_std"], 1)
                    link(dve.tensor_tensor(hn[:, :, :, :], hn[:, :, :, :], bc(st[:, :, :]), ALU.mult))
                    dve.tensor_tensor(hn[:, :, :, :].rearrange("p b h d -> p b (h d)"),
                                      hn[:, :, :, :].rearrange("p b h d -> p b (h d)"),
                                      col("outnorm", 0, D).unsqueeze(1).to_broadcast([128, NP, D]), ALU.mult)\
                        .then_inc(s["head_out"], 1)
                    dve.wait_ge(s["out_t"], 1)
                    dve.tensor_tensor(xg[:, :], xg[:, :], bank[1][:, :], ALU.add)

            run_stage("gated", LN + "rows_set gates qk rows columns neg_max weights attended head_out out_t f log exp_max decay "
                           "log_decay head_var head_std act dve", body)

        with nc.Fori(0, NG) as g:
            if "A" in stages:
                attention(g, False)
            else:
                def load(ctx, s, block):
                    @block.sync
                    def _(sp):
                        sp.dma_start(xg[:, :], x[g, :, :]).then_inc(s["x_in"], 16)
                        sp.dma_start(cg[:, :], ctxT[g, :, :]).then_inc(s["x_in"], 16)
                        sp.dma_start(ctk[:, :, :, :], ctx_tok[g, :, :, :, :]).then_inc(s["x_in"], 16)
                        sp.wait_ge(s["x_in"], 48)
                run_stage("load", "x_in", load)
            if "B" in stages:
                attention(g, True)
            if "C" in stages:
                moe0(g)
            if "D" in stages:
                delta(g)
            if "E" in stages:
                mlstm(g)
            if "F" in stages:
                moe1(g)

            def store(ctx, s, block):
                @block.sync
                def _(sp):
                    sp.dma_start(out[g, :, :], xg[:, :]).then_inc(s["stored"], 16)
                    sp.wait_ge(s["stored"], 16)
            run_stage("store", "stored", store)


def _layouts(i):
    f = {k: np.asarray(v) for k, v in i.items()}
    one = lambda v: v.reshape(-1, 1)

    def rows(v):
        return v.reshape(-1, 128).T

    def heads(v):
        out = np.zeros(v.shape[:-1] + (H, 32), np.float32)
        out[..., :8] = v.reshape(v.shape[:-1] + (H, 8))
        return out.reshape(v.shape[:-1] + (H * 32,))

    def down(v, p=128):
        out = np.zeros((128,) + v.shape[1:], np.float32)
        out[:v.shape[0]] = v
        return out

    def all_rows(v):
        return np.tile(v.reshape(1, -1), (128, 1))

    hk = f["L1_attn_beta_spike"].reshape(HD, 64)
    small = {
        "bq": rows(heads(f["L0_xattn_wq_b"])), "bk": rows(heads(f["L0_xattn_wk_b"])),
        "bv": rows(heads(f["L0_xattn_wv_b"])), "bo": one(f["L0_xattn_wo_b"]),
        "norm_in": one(f["L1_attn_norm_in_w"]), "conv_w": f["L1_attn_conv_w"].reshape(128, 4),
        "conv_b": one(f["L1_attn_conv_b"]), "bau": down(one(f["L1_attn_bau"])), "bad": rows(f["L1_attn_bad"]),
        "asp": rows(f["L1_attn_alpha_spike"].reshape(-1)), "bbeta": rows(np.repeat(f["L1_attn_bbeta"], 64)),
        "headw": rows(f["L1_attn_head_norm_w"].reshape(-1)), "bu1": down(one(f["L1_attn_bu1"])),
        "bu2": one(f["L1_attn_bu2"]), "ffw": one(f["L1_attn_ff_norm_w"]),
        "outnorm": all_rows(f["L1_xattn_outnorm_scale"]), "lng": one(f["L1_ffn_ln_g"]), "lnb": one(f["L1_ffn_ln_b"]),
        "rb": all_rows(f["L1_ffn_rb"]), "b1": rows(f["L1_ffn_b1"].reshape(-1)),
        "rank8": all_rows(np.arange(8, 0, -1, dtype=np.float32)),
        "gib": down(one(f["L1_xattn_igate_bias"])), "gfb": down(one(f["L1_xattn_fgate_bias"])),
        "rw0": f["L0_ffn_router_w"].T, "rw1": f["L1_ffn_rW"], "wau": f["L1_attn_Wau"], "wu1": f["L1_attn_Wu1"],
        "wu2": down(f["L1_attn_Wu2"]),
        "gates": np.concatenate([f["L1_xattn_igate_kernel"].reshape(3, 128, 4),
                                 f["L1_xattn_fgate_kernel"].reshape(3, 128, 4)], axis=2)
        .transpose(1, 0, 2).reshape(128, 24),
    }
    norm_rows = np.zeros((2, 64, 8, 8, 2), np.float32)
    for n in range(8):
        for a in range(2):
            norm_rows[a, :, n, n, a] = 1.0
    small["norm_rows"] = norm_rows
    norm_sel = norm_rows.transpose(3, 4, 2, 0, 1).reshape(16, 8, 128)
    small = np.concatenate([small[n].reshape(128, w) for n, w in SMALL], axis=1)

    blocks = np.zeros((128, 128), np.float32)
    blocks[:64, :64] = blocks[64:, 64:] = 1.0
    const = np.stack([np.full((128, 128), 1.0 / 128, np.float32), blocks, np.eye(128, dtype=np.float32)], axis=1)
    t = np.arange(64)
    causal = np.where(t[None, :] > t[:, None], np.float32(NEG), np.float32(0.0))
    causal_t = np.tile(causal.T, (2, 8))
    causal = np.tile(causal, (2, 8))
    j, q = np.arange(32)[:, None], np.arange(32)[None, :]
    level = [((j // (2 * c) == q // (2 * c)) & (j % (2 * c) < c) & (q % (2 * c) >= c)) for c in LEVELS] + [j == q]
    lmask = np.tile(np.stack(level, axis=1).astype(np.float32), (4, 1, 1))
    sel = np.zeros((8, 8, 128), np.float32)
    sel[np.arange(8), np.arange(8)] = 1.0

    w_self = np.stack([f["L0_attn_Wq"], f["L0_attn_Wk"], f["L0_attn_Wv"],
                       f["L0_attn_Wo"].reshape(8, 128, 128).transpose(1, 0, 2).reshape(128, 1024)], axis=1)
    wo = heads(f["L0_xattn_wo_w"]).T.reshape(4, 128, 128).transpose(1, 0, 2).reshape(128, 512)
    w_cross = np.stack([heads(f["L0_xattn_wq_w"].T), heads(f["L0_xattn_wk_w"].T), heads(f["L0_xattn_wv_w"].T), wo], axis=1)
    dn = np.zeros((E0, 384, 128), np.float32)
    dn[:, :I0] = f["L0_ffn_down_w"].transpose(0, 2, 1)
    w_moe0 = np.concatenate([f["L0_ffn_gate_w"].transpose(2, 0, 1), f["L0_ffn_up_w"].transpose(2, 0, 1),
                             dn.reshape(E0, 3, 128, 128).transpose(2, 0, 1, 3).reshape(128, E0, 384)], axis=2)
    beta_rep = np.repeat(f["L1_attn_Wbeta"], 64, axis=1)
    bsp = np.zeros((HDP, 2, 64, 2, 64), np.float32)
    for a in range(2):
        bsp[:, a, :, a, :] = hk.reshape(HDP, 2, 64)[:, a, :, None]
    bsp = bsp.reshape(HDP, 128, 128).transpose(1, 0, 2).reshape(128, 512)
    in_rows = lambda v: v.reshape(4, 128, 128).transpose(1, 0, 2).reshape(128, 512)
    wv = f["L1_attn_Wv"].reshape(128, HDP, 2, 64).transpose(0, 2, 1, 3).reshape(128, 512)
    w_delta = np.stack([f["L1_attn_Wq"], f["L1_attn_Wk"], wv, f["L1_attn_Wspike"], down(f["L1_attn_Wad"]), beta_rep,
                        bsp, in_rows(f["L1_attn_Wo"]), f["L1_attn_Wff1"], f["L1_attn_Wff3"], in_rows(f["L1_attn_Wff2"])],
                       axis=1)
    w_moe1 = np.concatenate([f["L1_ffn_W1"].transpose(1, 0, 2),
                             f["L1_ffn_W2"].reshape(E1, 2, 128, 128).transpose(2, 0, 1, 3).reshape(128, E1, 256)], axis=2)

    def grouped(v):
        return v.reshape(NG, T, D).transpose(0, 2, 1)

    ctx_tok = np.ones((NG, 128, NP, NHX, DHX + 1), np.float32)
    ctx_tok[..., :DHX] = f["ctx_1024"].reshape(NG, NP, 128, NHX, DHX).transpose(0, 2, 1, 3, 4)
    return {"x": grouped(f["x"]), "ctxT": grouped(f["ctx_1024"]), "ctx_tok": ctx_tok, "small": small, "const": const,
            "cmask": causal, "cmaskT": causal_t, "lmask": lmask, "sel": sel, "norm_sel": norm_sel, "w_self": w_self, "w_cross": w_cross, "w_moe0": w_moe0,
            "w_delta": w_delta, "w_moe1": w_moe1, "b2": f["L1_ffn_b2"]}


def kernel(**inputs):
    import concourse.bacc as _bacc
    from concourse.bass_utils import run_bass_kernel_spmd as _run

    nc = _bacc.Bacc("TRN2", target_bir_lowering=False, num_devices=1)
    arrays, args = {}, []
    for name, a in _layouts(inputs).items():
        a = np.ascontiguousarray(a)
        arrays[f"in_{name}_dram"] = a
        args.append(nc.dram_tensor(f"in_{name}_dram", a.shape, F32, kind="ExternalInput").ap())
    args.append(nc.dram_tensor("out_dram", (NG, D, T), F32, kind="ExternalOutput").ap())
    build(nc, *args)
    r = _run(nc, [arrays], core_ids=[0])
    return r.results[0]["out_dram"].transpose(0, 2, 1).reshape(B, S, D)
```
